# Optimizing a Trainium2 kernel written in Bass

```python
import numpy as np
import jax
import jax.numpy as jnp

def _softmax(x, axis=-1):
    return jax.nn.softmax(x, axis=axis)

def _gelu(x):
    return jax.nn.gelu(x, approximate=True)

def _silu(x):
    return jax.nn.silu(x)

def _sigmoid(x):
    return jax.nn.sigmoid(x)

def _layernorm(x, axis=-1, eps=1e-05):
    m = jnp.mean(x, axis=axis, keepdims=True)
    v = jnp.var(x, axis=axis, keepdims=True)
    return (x - m) / jnp.sqrt(v + eps)

def _scatter_add(tgt, idx, src, axis=0):
    return tgt.at[idx].add(src)

def _segment_sum(src, seg, n):
    return jax.ops.segment_sum(src, seg, n)
kernel_name = 'mk_decoder_postln_d1_seqx_r4_56aba6'

def setup_inputs(seed: int=0):
    np.random.seed(seed)
    _w = jnp.asarray

    def _rec_inputs():
        import jax
        import jax.numpy as jnp
        _rk = jax.random.key(seed)
        x = 7.22e-05 + 1 * jax.random.normal(jax.random.fold_in(_rk, 1), (16, 256, 256), jnp.float32)
        _lenS = 256 - jax.random.randint(jax.random.fold_in(_rk, 7), (16,), 0, max(1, 256 // 4) + 1, jnp.int32)
        _lenS2 = 120 - jax.random.randint(jax.random.fold_in(_rk, 8), (16,), 0, max(1, 120 // 4) + 1, jnp.int32)
        _ctx_1024P = jax.random.normal(jax.random.fold_in(_rk, 11), (16, 16, 256), jnp.float32)
        _ctx_1024c = jax.random.dirichlet(jax.random.fold_in(_rk, 511), 0.3 * jnp.ones((16,), jnp.float32), (16, 120))
        _ctx_1024t = jnp.einsum('bsk,bkd->bsd', _ctx_1024c, _ctx_1024P)
        _ctx_1024t = _ctx_1024t * jax.lax.rsqrt(jnp.mean(jnp.square(_ctx_1024t)) + 1e-12) * 0.953939
        ctx_1024 = -4.77421e-07 + 0.031248 * (_ctx_1024t + 0.3 * jax.random.normal(jax.random.fold_in(_rk, 611), (16, 120, 256), jnp.float32))
        return (x, ctx_1024)
    x, ctx_1024 = _rec_inputs()

    def _L0_attn_setup():
        import jax, jax.numpy as jnp
        import numpy as np
        EMBED = 256
        HEADS = 16
        HEAD_DIM = EMBED // HEADS
        RANK = 8
        ALPHA = 16
        SCALE_LORA = ALPHA / RANK

        def _lora_linear(x, W, b, A, B):
            return x @ W.T + b + SCALE_LORA * (x @ A.T @ B.T)
        key = jax.random.key(seed)
        ks = jax.random.split(key, 17)
        d = {'x': jax.random.normal(ks[0], (2, 512, EMBED), dtype=jnp.float32)}
        names = ['q', 'k', 'v', 'o']
        i = 1
        for n in names:
            d[f'W{n}'] = jax.random.normal(ks[i], (EMBED, EMBED), dtype=jnp.float32) * 0.02
            i += 1
            d[f'b{n}'] = jnp.zeros((EMBED,), dtype=jnp.float32)
            d[f'A{n}'] = jax.random.normal(ks[i], (RANK, EMBED), dtype=jnp.float32) * 0.02
            i += 1
            d[f'B{n}'] = jax.random.normal(ks[i], (EMBED, RANK), dtype=jnp.float32) * 0.02
            i += 1
        return d
    _L0_attn_all = _L0_attn_setup()
    _L0_attn_in = {k: v for k, v in _L0_attn_all.items() if k in ('Wq', 'bq', 'Aq', 'Bq', 'Wk', 'bk', 'Ak', 'Bk', 'Wv', 'bv', 'Av', 'Bv', 'Wo', 'bo', 'Ao', 'Bo')}
    del _L0_attn_all

    def _L0_xattn_setup():
        import jax, jax.numpy as jnp
        import numpy as np
        E, T, H, F = (8, 256, 256, 1024)
        key = jax.random.key(seed)
        k1, k2, k3 = jax.random.split(key, 3)
        x = jax.random.normal(k1, (E, T, H), dtype=jnp.float32)
        w1 = jax.random.normal(k2, (E, F, H), dtype=jnp.float32) * (1.0 / np.sqrt(H))
        w2 = jax.random.normal(k3, (E, F, H), dtype=jnp.float32) * (1.0 / np.sqrt(F))
        return {'x': x, 'w1': w1, 'w2': w2}
    _L0_xattn_all = _L0_xattn_setup()
    _L0_xattn_in = {k: v for k, v in _L0_xattn_all.items() if k in ()}
    del _L0_xattn_all

    def _L0_ffn_setup():
        import jax, jax.numpy as jnp
        import numpy as np
        TOP_K = 2
        key = jax.random.key(seed)
        k1, k2, k3, k4 = jax.random.split(key, 4)
        B, T, C, E = (4, 512, 256, 8)
        x = jax.random.normal(k1, (B, T, C), dtype=jnp.float32)
        Wg = jax.random.normal(k2, (C, E), dtype=jnp.float32) * 0.02
        W1 = jax.random.normal(k3, (E, C, 4 * C), dtype=jnp.float32) * 0.02
        W2 = jax.random.normal(k4, (E, 4 * C, C), dtype=jnp.float32) * 0.02
        return {'x': x, 'Wg': Wg, 'W1': W1, 'W2': W2}
    _L0_ffn_all = _L0_ffn_setup()
    _L0_ffn_in = {k: v for k, v in _L0_ffn_all.items() if k in ('Wg', 'W1', 'W2')}
    del _L0_ffn_all
    return {'x': x, 'ctx_1024': ctx_1024, 'L0_attn_Wq': _L0_attn_in['Wq'], 'L0_attn_bq': _L0_attn_in['bq'], 'L0_attn_Aq': _L0_attn_in['Aq'], 'L0_attn_Bq': _L0_attn_in['Bq'], 'L0_attn_Wk': _L0_attn_in['Wk'], 'L0_attn_bk': _L0_attn_in['bk'], 'L0_attn_Ak': _L0_attn_in['Ak'], 'L0_attn_Bk': _L0_attn_in['Bk'], 'L0_attn_Wv': _L0_attn_in['Wv'], 'L0_attn_bv': _L0_attn_in['bv'], 'L0_attn_Av': _L0_attn_in['Av'], 'L0_attn_Bv': _L0_attn_in['Bv'], 'L0_attn_Wo': _L0_attn_in['Wo'], 'L0_attn_bo': _L0_attn_in['bo'], 'L0_attn_Ao': _L0_attn_in['Ao'], 'L0_attn_Bo': _L0_attn_in['Bo'], 'L0_ffn_Wg': _L0_ffn_in['Wg'], 'L0_ffn_W1': _L0_ffn_in['W1'], 'L0_ffn_W2': _L0_ffn_in['W2']}

def reference(x, ctx_1024, L0_attn_Wq, L0_attn_bq, L0_attn_Aq, L0_attn_Bq, L0_attn_Wk, L0_attn_bk, L0_attn_Ak, L0_attn_Bk, L0_attn_Wv, L0_attn_bv, L0_attn_Av, L0_attn_Bv, L0_attn_Wo, L0_attn_bo, L0_attn_Ao, L0_attn_Bo, L0_ffn_Wg, L0_ffn_W1, L0_ffn_W2):
    import jax
    import jax.numpy as jnp

    def _L0_attn_ref(x, Wq, bq, Aq, Bq, Wk, bk, Ak, Bk, Wv, bv, Av, Bv, Wo, bo, Ao, Bo):
        import jax, jax.numpy as jnp
        import numpy as np
        EMBED = 256
        HEADS = 16
        HEAD_DIM = EMBED // HEADS
        RANK = 8
        ALPHA = 16
        SCALE_LORA = ALPHA / RANK

        def _lora_linear(x, W, b, A, B):
            return x @ W.T + b + SCALE_LORA * (x @ A.T @ B.T)
        N, S, _ = x.shape
        Q = _lora_linear(x, Wq, bq, Aq, Bq).reshape(N, S, HEADS, HEAD_DIM)
        K = _lora_linear(x, Wk, bk, Ak, Bk).reshape(N, S, HEADS, HEAD_DIM)
        V = _lora_linear(x, Wv, bv, Av, Bv).reshape(N, S, HEADS, HEAD_DIM)
        energy = jnp.einsum('nqhd,nkhd->nhqk', Q, K) / jnp.sqrt(jnp.float32(HEAD_DIM))
        attn = jax.nn.softmax(energy, axis=-1)
        out = jnp.einsum('nhqk,nkhd->nqhd', attn, V).reshape(N, S, EMBED)
        return _lora_linear(out, Wo, bo, Ao, Bo)

    def _L0_xattn_ref(x, w1, w2):
        import jax, jax.numpy as jnp
        import numpy as np
        E, T, H, F = (8, 256, 256, 1024)
        h = jnp.einsum('eth,efh->etf', x, w1)
        g = jax.nn.gelu(h, approximate=True)
        out = jnp.einsum('etf,efh->eth', g, w2)
        return out

    def _L0_ffn_ref(x, Wg, W1, W2):
        import jax, jax.numpy as jnp
        import numpy as np
        TOP_K = 2
        B, T, C = x.shape
        E = W1.shape[0]
        xf = x.reshape(-1, C)
        N = xf.shape[0]
        gate = jax.nn.softmax(xf @ Wg, axis=-1)
        top_w, top_i = jax.lax.top_k(gate, TOP_K)
        top_w = top_w / (top_w.sum(axis=-1, keepdims=True) + 1e-09)
        h = jnp.maximum(jnp.einsum('nc,ecf->nef', xf, W1), 0.0)
        y = jnp.einsum('nef,efc->nec', h, W2)
        comb = jnp.zeros((N, E), dtype=xf.dtype).at[jnp.arange(N)[:, None], top_i].add(top_w)
        out = jnp.einsum('nec,ne->nc', y, comb)
        return out.reshape(B, T, C)
    x = _layernorm(x + _L0_attn_ref(x, L0_attn_Wq, L0_attn_bq, L0_attn_Aq, L0_attn_Bq, L0_attn_Wk, L0_attn_bk, L0_attn_Ak, L0_attn_Bk, L0_attn_Wv, L0_attn_bv, L0_attn_Av, L0_attn_Bv, L0_attn_Wo, L0_attn_bo, L0_attn_Ao, L0_attn_Bo), axis=-1)
    x = _layernorm(x + _L0_xattn_ref(x, ctx_1024, ctx_1024), axis=-1)
    x = _layernorm(x + _L0_ffn_ref(x, L0_ffn_Wg, L0_ffn_W1, L0_ffn_W2), axis=-1)
    return x

_drawn_inputs = setup_inputs


def setup_inputs(seed=0):
    import zlib

    import numpy as np

    out = dict(_drawn_inputs(seed))
    spreads = {'L0_attn_bq': (0.0, 0.8),
     'L0_attn_bk': (0.0, 2.0),
     'L0_attn_bv': (0.0, 0.1),
     'L0_attn_bo': (0.0, 0.365)}
    factors = {'L0_attn_Wq': 8.0,
     'L0_attn_Aq': 8.0,
     'L0_attn_Bq': 8.0,
     'L0_attn_Wk': 8.0,
     'L0_attn_Ak': 8.0,
     'L0_attn_Bk': 8.0,
     'L0_attn_Wv': 6.314,
     'L0_attn_Av': 8.0,
     'L0_attn_Bv': 8.0,
     'L0_attn_Ao': 8.0,
     'L0_attn_Bo': 8.0}
    for name, (base, spread) in spreads.items():
        noise = np.random.default_rng([zlib.crc32(name.encode()), seed]).standard_normal(out[name].shape)
        drawn = base * np.exp(spread * noise) if base else spread * noise
        out[name] = jnp.asarray(drawn.astype(out[name].dtype))
    for name, factor in factors.items():
        out[name] = (out[name] * factor).astype(out[name].dtype)
    return out
```

```python
import concourse.bass as bass
from concourse import mybir
from contextlib import ExitStack


class Chain:

    def __init__(self, eng, sem, piece, steps):
        self.eng, self.sem, self.base, self.steps, self.n = eng, sem, piece * steps, steps, 0

    def __call__(self, ins, wait=None):
        self.n += 1
        assert self.n <= self.steps
        ins.then_inc(self.sem, 1)
        if wait:
            wait(self.eng, (self.sem, self.base + self.n))
        else:
            self.eng.wait_ge(self.sem, self.base + self.n)

    def end(self):
        assert self.n == self.steps, (self.n, self.steps)


class Stages:

    def __init__(self, i, batches):
        self.next = 0 <= i + 1 < batches
        self.cur = 0 <= i < batches
        self.post = 0 <= i - 1 < batches
        self.gate = 0 <= i - 2 < batches



def decoder_layer(nc, x, xT, ctx, ctxT, WqT, WkT, WvT, WoT, Aq, Ak, Av, Ao, BqT, BkT, BvT, BoT,
                  bq, bk, bv, bo, Wg, W1, W2, out):
    F32, F32R, F16 = mybir.dt.float32, mybir.dt.float32r, mybir.dt.float16
    I32, U32 = mybir.dt.int32, mybir.dt.uint32
    ALU, ACT, AX = mybir.AluOpType, mybir.ActivationFunctionType, mybir.AxisListType
    ds = bass.ds

    P = 128
    NB, T, C = x.shape
    S2 = ctx.shape[1]
    R = Aq.shape[0]
    LORA = 2.0
    D = 16
    H = C // D
    KC, TC = C // P, T // P
    HG = 4
    G = H // HG
    HR = P // HG
    MROW = 4 * D
    KROWS = MROW + 2
    E, F = W1.shape[0], W1.shape[2]
    FC = F // P
    N = NB * T
    NT = N // P
    ET = 256
    ETC = ET // P
    CAP = N + ET
    TILES = (2 * N + E * (ET - 1)) // ET
    ROW = C + 2
    DROP = 2 * N
    EPS = 1e-5
    XS, WS = 4.0, 16.0
    EXP_MASK, EXP_ONE = 0x7F800000, 1 << 23
    CUM = 288
    ROOT_BITS = 0x5F3759DF
    GELU_A, GELU_C = 0.044715, 0.7978845608028654

    x_tok = x.rearrange("b (c p) n -> b p c n", p=P)
    x_ch = xT.rearrange("b (k p) t -> b p k t", p=P)
    ctx_ch = ctxT.rearrange("b (k p) t -> b p k t", p=P)
    w1_e = W1.rearrange("e (k p) f -> e p k f", p=P)
    w2_e = W2.rearrange("e (c p) n -> e p c n", p=P)

    q_parts = nc.dram_tensor("q_parts", [H, 3, D, T], F32, kind="Internal").ap()
    k_parts = nc.dram_tensor("k_parts", [H, 2, D, T], F32, kind="Internal").ap()
    x2_rows = nc.dram_tensor("x2_rows", [N, C], F32, kind="Internal").ap()
    sent = nc.dram_tensor("sent", [E * CAP, ROW], F32, kind="Internal").ap()
    mixed = nc.dram_tensor("mixed", [2 * N, C], F32, kind="Internal").ap()
    q_rows = q_parts.rearrange("h s d t -> (s d) h t")
    k_rows = k_parts.rearrange("h s d t -> (s d) h t")

    es = ExitStack()
    with es:
        def sem(name):
            return es.enter_context(nc.semaphore(name))

        def pb(name):
            return es.enter_context(nc.psum_tensor(name, [P, 512], F32))

        top = [(nc.sbuf_base + 63) // 64 * 64]

        def sb(name, shape, dt):
            width = 2 if dt == F16 else 4
            for s in shape[1:]:
                width *= s
            t = nc.alloc_sbuf_tensor_at(name, shape, dt, offset=top[0])
            top[0] += (width + 31) // 32 * 32
            assert top[0] <= nc.sbuf_usable_end, (name, top[0])
            return t

        w_high = [sb("w1_high", [P, E, KC * F], F16), sb("w2_high", [P, E, FC * C], F16)]
        w_low = [sb("w1_low", [P, E, KC * F], F16), sb("w2_low", [P, E, FC * C], F16)]
        ident = sb("ident", [P, P], F32)
        ones_sq = sb("ones_sq", [P, P], F16)
        before = sb("before", [P, P], F16)
        iota_e = sb("iota_e", [P, E], F32)
        yscale = sb("yscale", [P, E], F32)
        count = sb("count", [P, E], F32)
        logits = sb("logits", [P, NT, E], F32)
        picked = sb("picked", [P, 2, NT], F32)
        weight = sb("weight", [P, 2, NT], F32)
        token = sb("token", [P, TC], F32)
        phase = top[0]

        wq = sb("wq", [P, KC, C], F32)
        wk = sb("wk", [P, KC, C], F32)
        wv = sb("wv", [P, KC, C], F32)
        wo = sb("wo", [P, G, C], F32)
        bqk = sb("bqk", [P, 2, KC], F32)
        bv_all = sb("bv_all", [P, C], F32)
        wg = sb("wg", [P, KC, E], F32)
        staging = top[0]
        xT_sb = sb("xT_sb", [P, KC, T], F32)
        part = sb("part", [P, 4, T], F32R)
        qs = sb("qs", [P, G, HG, T], F32R)
        ks = sb("ks", [P, G, HG, T], F32R)
        pt = sb("pt", [P, HG, TC * T], F32)
        va = sb("va", [P, TC, H, HR], F32)
        mx = sb("mx", [P, TC, HG], F32)
        mm = sb("mm", [P, TC, 2 * HG], F32R)
        mT = sb("mT", [2 * HG, T], F32)
        on = sb("on", [P, G, T], F32)
        x1 = sb("x1", [P, TC, C], F32)
        x1T = sb("x1T", [P, KC, T], F32)
        x2T, hv, hu = x1T, x1T[0:S2, 0, :], x1T[0:S2, 1, :]
        cT = sb("cT", [P, KC, S2], F32)
        cr = sb("cr", [S2, C], F32)
        x2 = sb("x2", [P, TC, ROW], F32)
        bn = sb("bn", [P, 2, TC, 6], F32)
        mv = sb("mv", [P, 2, TC, 2], F32)
        rstd = sb("rstd", [P, 2, TC, 2], F32)
        root = sb("root", [P, 2, TC, 1], F32)
        lg = sb("lg", [P, TC, E], F32)
        lg8 = sb("lg8", [P, TC, 8], F32)
        ix8 = sb("ix8", [P, TC, 8], U32)
        pick = sb("pick", [P, 2, TC, E], F32)
        mask = sb("mask", [P, TC, E], F16)
        cum = sb("cum", [P, TC + 1, E], F32)
        seat = sb("seat", [P, TC, E], F32)
        seat_k = sb("seat_k", [P, 2, TC], F32)
        seat_i = sb("seat_i", [P, 2, TC], I32)

        top[0] = staging
        stage = [sb(f"stage{i}", [P, 2, KC * F], F32) for i in range(2)]
        lora_a = sb("lora_a", [R, 3, C], F32)
        lora_ao = sb("lora_ao", [R, G, P], F32)
        lora_b = sb("lora_b", [R, 4, C], F32)
        absmax = sb("absmax", [P, 2], F32)
        peak = sb("peak", [2, 1], F32)
        diag = sb("diag", [2, 2], F32)
        ones_2 = sb("ones_2", [2, P], F32)
        wpow = sb("wpow", [P, 2 * E], F32)
        winv = sb("winv", [P, 2 * E], F32)

        top[0] = phase
        xt = sb("xt", [P, ETC, ROW], F32)
        xs = [sb(n, [P, KC, ET], F16) for n in ("xs_high", "xs_low")]
        hs = [sb(n, [P, FC, ET], F16) for n in ("hs_high", "hs_low")]
        ys = sb("ys", [P, ETC, C], F32)
        meta_next = sb("meta_next", [P, ETC, 2], F32)
        other = sb("other", [P, ETC], F32)
        dest = sb("dest", [P, ETC], I32)
        fx = sb("fx", [P, NT, C], F32)
        fy = [sb(f"fy{i}", [P, 2, TC, C], F32) for i in range(2)]
        fo = [sb(f"fo{i}", [P, TC, C], F32) for i in range(2)]
        fbn = sb("fbn", [P, 2, TC, 6], F32)
        fmv = sb("fmv", [P, 2, TC, 2], F32)
        frs = sb("frs", [P, 2, TC, 2], F32)
        froot = sb("froot", [P, 2, TC, 1], F32)
        pad = sb("pad", [P, ETC, ROW], F32)
        fulls = sb("fulls", [P, FC * 2], F32)
        over = sb("over", [P, E, FC * 2], F32)
        num = sb("num", [P, E], F32)
        tiles_of = sb("tiles_of", [P, E], F32)
        last_of = sb("last_of", [P, E], F32)
        base_of = sb("base_of", [P, E], F32)
        ones_e = sb("ones_e", [P, E], F32)
        tau = sb("tau", [P, TILES], F32)
        by_e = sb("by_e", [P, TILES, E], F32)
        tile_e = sb("tile_e", [P, TILES], F32)
        tile_row = sb("tile_row", [P, TILES], F32)
        tab = sb("tab", [P, 2, TILES], I32)
        cnt_i = sb("cnt_i", [P, E], I32)
        chosen = sb("chosen", [P, 2, NT, E], F32)
        gmax = sb("gmax", [P, NT], F32)
        gate = sb("gate", [P, NT, E], F32)
        gprod = sb("gprod", [P, 2, NT, E], F32)
        gscale = sb("gscale", [P, 2, NT], F32)
        gsum = sb("gsum", [P, NT], F32)
        assert N // ET == FC * 2

        S = [pb(f"S{i}") for i in range(2)]
        ST = [pb(f"ST{i}") for i in range(2)]
        PV = [pb(f"PV{i}") for i in range(2)]
        M = [pb(f"M{i}") for i in range(2)]
        HB = [S[0], S[1], ST[0], ST[1]]
        YB, XB = PV, M[0]

        const_ready = sem("const_ready")
        lora_loaded = sem("lora_loaded")
        wo_loaded = sem("wo_loaded")
        lora_done = sem("lora_done")
        fold_chain = sem("fold_chain")
        fold_done = sem("fold_done")
        stage_loaded = [sem(f"stage_loaded{i}") for i in range(2)]
        absmax_done = sem("absmax_done")
        absmax_turned = sem("absmax_turned")
        diag_chain = sem("diag_chain")
        diag_done = sem("diag_done")
        peak_spread = sem("peak_spread")
        scale_chain = sem("scale_chain")
        scale_done = sem("scale_done")
        high_done = sem("high_done")
        low_done = sem("low_done")
        rows_const = sem("rows_const")
        xT_loaded = sem("xT_loaded")
        x_loaded = sem("x_loaded")
        cT_loaded = sem("cT_loaded")
        cr_loaded = sem("cr_loaded")
        qk_proj = sem("qk_proj")
        qk_high = sem("qk_high")
        qk_low = sem("qk_low")
        part_sent = [sem(f"part_sent{m}") for m in range(KC)]
        slot_loaded = [sem(f"slot_loaded{g}") for g in range(G)]
        mrow_zero = sem("mrow_zero")
        mrow_set = [sem(f"mrow_set{g}") for g in range(G)]
        v_proj = sem("v_proj")
        v_ready = sem("v_ready")
        s_done = sem("s_done")
        max_done = sem("max_done")
        msplit = sem("msplit")
        mT_done = sem("mT_done")
        mT_copied = sem("mT_copied")
        st_done = sem("st_done")
        exp_done = sem("exp_done")
        pv_done = sem("pv_done")
        den_ready = sem("den_ready")
        norm_done = sem("norm_done")
        o_done = sem("o_done")
        z1_done = sem("z1_done")
        ln1_stats = sem("ln1_stats")
        x1_ready = sem("x1_ready")
        x1T_done = sem("x1T_done")
        x1T_copied = sem("x1T_copied")
        mid_done = sem("mid_done")
        h_copied = sem("h_copied")
        gelu_in = sem("gelu_in")
        tanh_done = sem("tanh_done")
        gelu_out = sem("gelu_out")
        xo_done = sem("xo_done")
        z2_done = sem("z2_done")
        ln2_stats = sem("ln2_stats")
        x2_ready = sem("x2_ready")
        x2T_done = sem("x2T_done")
        x2T_copied = sem("x2T_copied")
        x2_stored = sem("x2_stored")
        lg_done = sem("lg_done")
        lg_copied = sem("lg_copied")
        choice = sem("choice")
        cum_copied = sem("cum_copied")
        seat_chain = sem("seat_chain")
        rows_sent = sem("rows_sent")
        post_const = sem("post_const")
        table = sem("table")
        pad_sent = sem("pad_sent")
        gating = sem("gating")
        gate_exp = sem("gate_exp")
        tile_loaded = sem("tile_loaded")
        turned = sem("turned")
        xs_high_done = sem("xs_high_done")
        xs_low_done = sem("xs_low_done")
        up_done = sem("up_done")
        hid_high = sem("hid_high")
        hid_low = sem("hid_low")
        down_done = sem("down_done")
        meta_chain = sem("meta_chain")
        dest_ready = sem("dest_ready")
        y_copied = sem("y_copied")
        y_sent = sem("y_sent")
        fin_loaded = [sem(f"fin_loaded{i}") for i in range(2)]
        fx_loaded = sem("fx_loaded")
        fin_chain = sem("fin_chain")
        fin_ready = sem("fin_ready")
        fin_stored = [sem(f"fin_stored{i}") for i in range(2)]

        FOLDS = 4
        CHOICE_STEPS, SEAT_STEPS, TABLE_STEPS = 6, 5, 14
        NEWTON = 3
        NORM_STEPS = 2 + 2 + 3 * NEWTON + 1
        FIN_STEPS = 2 + NORM_STEPS

        block = es.enter_context(nc.Block())

        def wait(eng, s, value):
            if not isinstance(value, int) or value > 0:
                eng.wait_ge(s, value)

        def pipeline(eng, body):
            for i in range(-1, 3):
                body(i, Stages(i, NB))
            with eng.Fori(0, NB - 4, 1) as n:
                body(n + 3, Stages(3, NB))
            for i in range(NB - 1, NB + 2):
                body(i, Stages(i, NB))

        def wait_apart(eng, *waits):
            values = [(s, v if isinstance(v, int) else eng.to_reg(v)) for s, v in waits]
            eng.wait_ge(const_ready, 1)
            for s, value in values:
                wait(eng, s, value)

        def at(v, n):
            return v[n] if isinstance(n, int) else v[ds(n, 1)][0]

        def row_of(t, n):
            return t[:, n, :] if isinstance(n, int) else t[:, ds(n, 1), :].rearrange("p a n -> p (a n)")

        def min_of(n):
            return min(n, NB) if isinstance(n, int) else n

        def scored(i, g, st):
            return (i, g + 1, st.cur) if g < G - 1 else (i + 1, 0, st.next)

        @block.sync
        def _(sp):
            for w_sb, w in ((wq, WqT), (wk, WkT), (wv, WvT)):
                sp.dma_start(w_sb[:, :, :], w.rearrange("(k p) n -> p k n", p=P)).then_inc(lora_loaded, 16)
            sp.dma_start(bqk[:, 0, :], bq).then_inc(lora_loaded, 16)
            sp.dma_start(bqk[:, 1, :], bk).then_inc(lora_loaded, 16)
            sp.dma_start(bv_all[:, :], bv.rearrange("(a n) -> a n", a=1).to_broadcast([P, C])).then_inc(lora_loaded, 16)
            sp.dma_start(wg[:, :, :], Wg.rearrange("(k p) e -> p k e", p=P)).then_inc(lora_loaded, 16)
            for n, a in enumerate((Aq, Ak, Av)):
                sp.dma_start(lora_a[:, n, :], a).then_inc(lora_loaded, 16)
            for n, b in enumerate((BqT, BkT, BvT, BoT)):
                sp.dma_start(lora_b[:, n, :], b).then_inc(lora_loaded, 16)
            sp.wait_ge(const_ready, 1)
            wo_v = WoT.rearrange("(g j d) n -> j d g n", g=G, j=HG)
            for j in range(HG):
                sp.dma_start(wo[j * HR:j * HR + D, :, :], wo_v[j]).then_inc(wo_loaded, 16)
            sp.dma_start(wo[D:D + 1, 0, :], bo.rearrange("(a n) -> a n", a=1)).then_inc(wo_loaded, 16)
            sp.dma_start(lora_ao[:, :, :].rearrange("r g (j z) -> r (g j) z", z=HR)[:, :, 0:D],
                         Ao.rearrange("r (h d) -> r h d", d=D)).then_inc(wo_loaded, 16)
            for e in range(E):
                if e >= 2:
                    sp.wait_ge(low_done, 2 * (e - 1))
                sp.dma_start(stage[e % 2][:, 0, :].rearrange("p (k f) -> p k f", k=KC), w1_e[e]).then_inc(stage_loaded[e % 2], 16)
                sp.dma_start(stage[e % 2][:, 1, :].rearrange("p (k f) -> p k f", k=FC), w2_e[e]).then_inc(stage_loaded[e % 2], 16)
            sp.wait_ge(low_done, 2 * E)
            sp.wait_ge(scale_done, E + 1)
            sp.wait_ge(fold_done, FOLDS)

            def body(i, st):
                b = i + 1
                if st.next:
                    wait(sp, v_proj, b)
                    sp.dma_start(xT_sb[:, :, :], at(x_ch, b)).then_inc(xT_loaded, 16)
                if st.post:
                    wait(sp, xo_done, i - 1)
                    sp.dma_start(cT[:, :, :], at(ctx_ch, i - 1)).then_inc(cT_loaded, 16)
                    sp.dma_start(cr[:, :], at(ctx, i - 1)).then_inc(cr_loaded, 16)
                for g in range(G):
                    if st.next and g < KC:
                        wait_apart(sp, (qk_low, KC * b + g + 1), *((slot_loaded[gg], 64 * b) for gg in (2 * g, 2 * g + 1)))
                        heads = slice(g * P // D, (g + 1) * P // D)
                        for scratch, s, src in ((q_parts, 0, 0), (q_parts, 1, 1), (q_parts, 2, 0),
                                                (k_parts, 0, 2), (k_parts, 1, 3)):
                            sp.dma_start(scratch[heads, s], part[:, src, :].bitcast(F32)).then_inc(part_sent[g], 16)
                    if g == 0 and (st.gate or st.post):
                        wait(sp, x2_ready, min_of(i - 1))
                    if g == 0 and st.post:
                        sp.dma_start(x1[:, :, :], at(x_tok, i - 1)).then_inc(x_loaded, 16)
                    if g == 0 and st.gate:
                        x2_v = x2_rows.rearrange("(b c p) n -> b p c n", p=P, c=TC)
                        sp.dma_start(at(x2_v, i - 2), x2[:, :, 0:C]).then_inc(x2_stored, 16)
                    if st.next:
                        wait_apart(sp, (part_sent[g // 2], 80 * (b + 1)), (st_done, H * i + HG * (g + 1)))
                        hd = slice(g * HG, (g + 1) * HG)
                        for dst, row, src in ((qs, 0, q_rows[0:2 * D, hd]), (qs, 2 * D, q_rows[D:3 * D, hd]),
                                              (ks, 0, k_rows[:, hd]), (ks, 2 * D, k_rows[:, hd])):
                            sp.dma_start(dst[row:row + 2 * D, g, :, :].bitcast(F32), src).then_inc(slot_loaded[g], 16)
            pipeline(sp, body)

            def load_tile(t):
                row = sp.value_load(tab[0:1, 1, t:t + 1] if isinstance(t, int) else tab[0:1, 1, ds(t, 1)],
                                    min_val=0, max_val=E * CAP - ET)
                sp.dma_start(xt[:, :, :], sent[ds(row, ET), :].rearrange("(c p) n -> p c n", p=P)).then_inc(tile_loaded, 16)
            sp.wait_ge(x2_stored, 16 * NB)
            sp.wait_ge(rows_sent, 64 * NB)
            sp.dma_start(fx[:, :, :], x2_rows.rearrange("(c p) n -> p c n", p=P)).then_inc(fx_loaded, 16)
            sp.wait_ge(table, TABLE_STEPS)
            sp.wait_ge(pad_sent, 16 * E)
            load_tile(0)
            with sp.Fori(0, TILES - 1, 1) as t:
                sp.wait_ge(turned, t + 1)
                sp.wait_ge(meta_chain, 2 * t + 1)
                load_tile(t + 1)

            sp.wait_ge(y_sent, 16 * ETC * TILES)
            fin_y = [mixed[k * N:(k + 1) * N, :].rearrange("(b c p) n -> b p c n", p=P, c=TC) for k in range(2)]
            out_v = out.rearrange("b (c p) n -> b p c n", p=P)

            def load_fin(n, q):
                b = n * 2 + q
                for k in range(2):
                    sp.dma_start(fy[q][:, k, :, :], at(fin_y[k], b)).then_inc(fin_loaded[q], 16)

            def store_fin(n, q):
                b = n * 2 + q
                sp.wait_ge(fin_ready, TC * (b + 1))
                sp.dma_start(at(out_v, b), fo[q][:, :, :]).then_inc(fin_stored[q], 16)
            load_fin(0, 0)
            load_fin(0, 1)
            with sp.Fori(0, NB // 2 - 1, 1) as n:
                for q in range(2):
                    store_fin(n, q)
                    load_fin(n + 1, q)
            for q in range(2):
                store_fin(NB // 2 - 1, q)
            for q in range(2):
                sp.wait_ge(fin_stored[q], 16 * NB // 2)

        @block.gpsimd
        def _(pool):
            g = nc.gpsimd
            g.memset(wo[:, :, :], 0.0)
            g.memset(ident[:, :], 0.0)
            g.memset(before[:, :], 1.0)
            g.memset(ones_sq[:, :], 1.0)
            g.memset(ones_2[:, :], 1.0)
            g.iota(iota_e[:, :], pattern=[[1, E]], base=0, channel_multiplier=0, allow_small_or_imprecise_dtypes=True)
            g.iota(count[:, :], pattern=[[CAP, E]], base=0, channel_multiplier=0, allow_small_or_imprecise_dtypes=True)
            g.iota(token[:, :], pattern=[[P, TC]], base=0, channel_multiplier=1, allow_small_or_imprecise_dtypes=True)
            g.memset(lora_ao[:, :, :], 0.0).then_inc(const_ready, 1)
            pool.wait_ge(const_ready, 1)
            g.affine_select(out=ident[:, :], in_=ident[:, :], compare_op=ALU.not_equal, fill=1.0,
                            base=0, pattern=[[-1, P]], channel_multiplier=1)
            g.affine_select(out=before[:, :], in_=before[:, :], compare_op=ALU.is_gt, fill=0.0,
                            base=0, pattern=[[1, P]], channel_multiplier=-1).then_inc(const_ready, 1)
            pool.wait_ge(low_done, 2 * E)
            pool.wait_ge(scale_done, E + 1)
            pool.wait_ge(fold_done, FOLDS)
            g.memset(ks[MROW:KROWS, :, :, :].bitcast(F32), 1.0).then_inc(rows_const, 1)
            pool.wait_ge(rows_const, 1)
            g.memset(va[:, :, :, D:HR], 1.0).then_inc(rows_const, 1)
            pool.wait_ge(rows_const, 2)

            def body(i, st):
                for gr in range(G):
                    if st.next:
                        wait_apart(pool, (st_done, H * i + HG * (gr + 1)))
                        g.memset(qs[MROW:KROWS, gr, :, :].bitcast(F32), 0.0).then_inc(mrow_zero, 1)
                        zeroed = [(mrow_zero, G * (i + 1) + gr + 1)]
                    else:
                        zeroed = []
                    if gr == 2 and st.post:
                        wait_apart(pool, (h_copied, i), *zeroed)
                        link = Chain(pool, gelu_in, i - 1, 3)
                        link(g.tensor_tensor(hu, hv, hv, ALU.mult), wait_apart)
                        link(g.tensor_scalar(hu, hu, GELU_A, 1.0, ALU.mult, ALU.add), wait_apart)
                        link(g.tensor_tensor(hu, hu, hv, ALU.mult), wait_apart)
                    if gr == 3 and st.post:
                        wait_apart(pool, (tanh_done, i), *zeroed)
                        link = Chain(pool, gelu_out, i - 1, 2)
                        link(g.tensor_scalar(hu, hu, 1.0, None, ALU.add), wait_apart)
                        link(g.tensor_tensor(hv, hu, hv, ALU.mult), wait_apart)
                    if gr == 3 and st.gate:
                        wait_apart(pool, (x2_ready, i - 1), (choice, CHOICE_STEPS * (i - 1)), (seat_chain, SEAT_STEPS * (i - 1)))
                        for k in range(2):
                            for c in range(TC):
                                g.indirect_dma_start(
                                    out=sent, out_offset=bass.IndirectOffsetOnAxis(seat_i[:, k, c:c + 1], 0),
                                    in_=x2[:, c, :], in_offset=None).then_inc(rows_sent, 16)
            pipeline(pool, body)

            pool.wait_ge(rows_sent, 64 * NB)
            g.memset(pad[:, :, :], 0.0).then_inc(post_const, 1)
            pool.wait_ge(post_const, 1)
            g.memset(pad[:, :, C:C + 1], float(DROP))
            g.memset(ones_e[:, :], 1.0)
            g.iota(fulls[:, :], pattern=[[ET, N // ET]], base=0, channel_multiplier=0, allow_small_or_imprecise_dtypes=True)
            g.iota(tau[:, :], pattern=[[1, TILES]], base=0, channel_multiplier=0,
                   allow_small_or_imprecise_dtypes=True).then_inc(post_const, 1)
            pool.wait_ge(table, TABLE_STEPS)
            pool.wait_ge(post_const, 2)
            for e in range(E):
                row = pool.value_load(cnt_i[0:1, e:e + 1], min_val=0, max_val=E * CAP - ET)
                pool.dma_start(sent[ds(row, ET), :].rearrange("(c p) n -> p c n", p=P), pad[:, :, :]).then_inc(pad_sent, 16)

            with pool.Fori(0, TILES, 1) as t:
                wait_apart(pool, (y_copied, t + 1), (dest_ready, t + 1))
                for c in range(ETC):
                    g.indirect_dma_start(
                        out=mixed, out_offset=bass.IndirectOffsetOnAxis(dest[:, c:c + 1], 0),
                        in_=ys[:, c, :], in_offset=None, bounds_check=2 * N - 1, oob_is_err=False).then_inc(y_sent, 16)

        @block.scalar
        def _(act):
            a = nc.scalar
            for e in range(E):
                act.wait_ge(scale_done, e + 1)
                for w in range(2):
                    a.activation(w_high[w][:, e, :], stage[e % 2][:, w, :], ACT.Identity,
                                 scale=winv[:, 2 * e + w:2 * e + w + 1]).then_inc(high_done, 1)

            def body(i, st):
                b = i + 1
                for g in range(G):
                    sb_, sg, s_on = scored(i, g, st)
                    for j in range(HG):
                        if st.cur:
                            act.wait_ge(st_done, H * i + HG * g + j + 1)
                            wait(act, pv_done, G * i + g)
                            a.activation(pt[:, j, :], ST[j % 2][:, :], ACT.Exp).then_inc(exp_done, 1)
                        if j == 1 and g == 0 and st.gate:
                            act.wait_ge(ln2_stats, NORM_STEPS * (i - 1))
                            wait(act, x2_stored, 16 * (i - 2))
                            wait(act, rows_sent, 64 * (i - 2))
                            for c in range(TC):
                                last = a.activation(x2[:, c, 0:C], x1[:, c, :], ACT.Identity, bias=rstd[:, 1, c, 1:2],
                                                    scale=rstd[:, 1, c, 0:1])
                            last.then_inc(x2_ready, 1)
                        if j == 1 and g == 3 and st.post:
                            act.wait_ge(gelu_in, 3 * i)
                            a.activation(hu, hu, ACT.Tanh, scale=GELU_C).then_inc(tanh_done, 1)
                    if g < KC and st.next:
                        act.wait_ge(qk_proj, KC * b + g + 1)
                        wait(act, part_sent[1 - g], 80 * (b + g))
                        for n in range(2):
                            last = a.activation(part[:, 2 * n, :], M[0][:, n * T:(n + 1) * T], ACT.Identity,
                                                bias=bqk[:, n, g:g + 1])
                        last.then_inc(qk_high, 1)
                    if g == 2 and st.post:
                        act.wait_ge(ln1_stats, NORM_STEPS * i)
                        for c in range(TC):
                            last = a.activation(x1[:, c, :], x1[:, c, :], ACT.Identity, bias=rstd[:, 0, c, 1:2],
                                                scale=rstd[:, 0, c, 0:1])
                        last.then_inc(x1_ready, 1)
                        act.wait_ge(x1T_done, i)
                        a.activation(x1T[:, :, :].rearrange("p k t -> p (k t)"), M[0][:, :], ACT.Copy).then_inc(x1T_copied, 1)
                    if s_on:
                        act.wait_ge(mT_done, G * sb_ + sg + 1)
                        wait(act, mrow_set[sg - 1], 16 * (sb_ + 1) if sg else 16 * sb_)
                        a.activation(mT[:, :], M[1][0:2 * HG, 0:T], ACT.Copy).then_inc(mT_copied, 1)
                        act.wait_ge(mT_copied, G * sb_ + sg + 1)
                        act.dma_start(qs[MROW:KROWS, sg, :, :].bitcast(F32), mT[:, :]).then_inc(mrow_set[sg], 16)
                    if g == 1 and st.gate:
                        act.wait_ge(lg_done, i - 1)
                        wait(act, choice, CHOICE_STEPS * (i - 2))
                        a.activation(lg[:, :, :].rearrange("p c e -> p (c e)"), M[1][:, T:T + TC * E], ACT.Copy).then_inc(lg_copied, 1)
                    if g == 0 and st.gate:
                        act.wait_ge(x2T_done, i - 1)
                        a.activation(x2T[:, :, :].rearrange("p k t -> p (k t)"), M[1][:, :], ACT.Copy).then_inc(x2T_copied, 1)
                    if g == 2 and (st.post or st.gate):
                        act.wait_ge(mid_done, i)
                    if g == 2 and st.gate:
                        wait(act, seat_chain, SEAT_STEPS * (i - 2))
                        a.activation(cum[:, :, :].rearrange("p c e -> p (c e)"), M[1][:, CUM:CUM + 3 * E], ACT.Copy).then_inc(cum_copied, 1)
                    if g == 2 and st.post:
                        a.activation(hv, M[1][0:S2, 0:T], ACT.Copy).then_inc(h_copied, 1)
            pipeline(act, body)

            act.wait_ge(gating, 3)
            a.activation(gate[:, :, :], gate[:, :, :], ACT.Exp).then_inc(gate_exp, 1)

            def turn(t):
                act.wait_ge(turned, t + 1)
                a.activation(xs[0][:, :, :].rearrange("p k t -> p (k t)"), XB[:, :], ACT.Copy, scale=XS).then_inc(xs_high_done, 1)

            def tile(t, more):
                for q in range(FC // 2):
                    act.wait_ge(up_done, FC // 2 * t + q + 1)
                    a.activation(hs[0][:, 2 * q:2 * q + 2, :].rearrange("p f t -> p (f t)"), HB[q][:, :], ACT.Relu).then_inc(hid_high, 1)
                if more:
                    turn(t + 1)
                act.wait_ge(down_done, t + 1)
                wait(act, y_sent, 16 * ETC * t)
                for c in range(ETC):
                    last = a.activation(ys[:, c, :], YB[c][:, 0:C], ACT.Copy)
                last.then_inc(y_copied, 1)
            turn(0)
            tile(0, True)
            with act.Fori(0, TILES - 2, 1) as t:
                tile(t + 1, True)
            tile(TILES - 1, False)

            def fin(n, q):
                act.wait_ge(fin_chain, FIN_STEPS * (2 * n + q + 1))
                wait(act, fin_stored[q], 16 * n)
                for c in range(TC):
                    a.activation(fo[q][:, c, :], row_of(fx, 2 * (2 * n + q) + c), ACT.Identity, bias=frs[:, q, c, 1:2],
                                 scale=frs[:, q, c, 0:1]).then_inc(fin_ready, 1)
            for q in range(2):
                fin(0, q)
            with act.Fori(0, NB // 2 - 1, 1) as n:
                for q in range(2):
                    fin(n + 1, q)

        @block.vector
        def _(dve):
            v = nc.vector
            dve.wait_ge(lora_loaded, 16 * 14)
            dve.wait_ge(wo_loaded, 16 * 6)
            for n, w_sb in enumerate((wq, wk, wv)):
                dve.wait_ge(lora_done, n + 1)
                flat = w_sb[:, :, :].rearrange("p k n -> p (k n)")
                last = v.scalar_tensor_tensor(flat, (S[0], S[1], ST[0])[n][:, :], LORA, flat, ALU.mult, ALU.add)
                if n:
                    last.then_inc(fold_done, 1)
                else:
                    link = Chain(dve, fold_chain, 0, 1)
                    link(last)
                    v.tensor_scalar(flat, flat, float(D) ** -0.5, None, ALU.mult)
                    v.tensor_scalar(bqk[:, 0, :], bqk[:, 0, :], float(D) ** -0.5, None, ALU.mult).then_inc(fold_done, 1)
            dve.wait_ge(lora_done, 4)
            for n, bank in enumerate((ST[1], PV[0])):
                flat = wo[:, 2 * n:2 * n + 2, :].rearrange("p k n -> p (k n)")
                last = v.scalar_tensor_tensor(flat, bank[:, :], LORA, flat, ALU.mult, ALU.add)
            last.then_inc(fold_done, 1)
            for e in range(E):
                dve.wait_ge(stage_loaded[e % 2], 32 * (e // 2 + 1))
                v.tensor_reduce(absmax[:, :], stage[e % 2][:, :, :], AX.X, ALU.max, apply_absolute_value=True).then_inc(absmax_done, 1)
                link = Chain(dve, diag_chain, e, 1)
                dve.wait_ge(absmax_turned, e + 1)
                link(v.tensor_reduce(peak[:, :], M[0][0:2, 0:P], AX.X, ALU.max))
                v.tensor_scalar(diag[:, :], ident[0:2, 0:2], peak[:, 0:1], None, ALU.mult).then_inc(diag_done, 1)
                dve.wait_ge(peak_spread, e + 1)
                link = Chain(dve, scale_chain, e, 2)
                pw = wpow[:, 2 * e:2 * e + 2]
                link(v.tensor_scalar(pw, M[1][:, 0:2], 2.0 ** -60, None, ALU.max))
                link(v.tensor_scalar(pw.bitcast(I32), pw.bitcast(I32), EXP_MASK, None, ALU.bitwise_and))
                v.tensor_scalar(winv[:, 2 * e:2 * e + 2].bitcast(I32), pw.bitcast(I32), -1.0, float((254 + 4) * EXP_ONE),
                                ALU.mult, ALU.add).then_inc(scale_done, 1)
                for w in range(2):
                    dve.wait_ge(high_done, 2 * e + w + 1)
                    v.scalar_tensor_tensor(w_low[w][:, e, :], stage[e % 2][:, w, :], winv[:, 2 * e + w:2 * e + w + 1],
                                           w_high[w][:, e, :], ALU.mult, ALU.subtract).then_inc(low_done, 1)
            pw_v = wpow[:, :].rearrange("p (e w) -> p e w", w=2)
            v.scalar_tensor_tensor(yscale[:, :], pw_v[:, :, 0], 1.0 / (XS * WS * WS), pw_v[:, :, 1],
                                   ALU.mult, ALU.mult).then_inc(scale_done, 1)

            def scale_and_shift(link, stats, to, tmp):
                var, r = stats[:, :, 1:2], to[:, :, 0:1]
                link(v.tensor_scalar(var, var, EPS, None, ALU.add))
                link(v.tensor_scalar(r.bitcast(I32), var.bitcast(I32), -0.5, float(ROOT_BITS), ALU.mult, ALU.add))
                for _ in range(NEWTON):
                    link(v.scalar_tensor_tensor(tmp, r, -0.5, r, ALU.mult, ALU.mult))
                    link(v.tensor_tensor(tmp, tmp, var, ALU.mult))
                    link(v.scalar_tensor_tensor(r, tmp, 1.5, r, ALU.add, ALU.mult))
                link(v.scalar_tensor_tensor(to[:, :, 1:2], stats[:, :, 0:1], -1.0, r, ALU.mult, ALU.mult))

            def norm_stats(eng_sem, piece, z, which):
                link = Chain(dve, eng_sem, piece, NORM_STEPS)
                for c in range(TC):
                    last = v.bn_stats(bn[:, which, c, :], z[:, c, :])
                link(last, wait_apart)
                for c in range(TC):
                    last = v.bn_aggr(mv[:, which, c, :], bn[:, which, c, :])
                link(last)
                scale_and_shift(link, mv[:, which], rstd[:, which], root[:, which])
                link.end()

            def body(i, st):
                b = i + 1
                for g in range(G):
                    sb_, sg, s_on = scored(i, g, st)
                    if s_on:
                        for j in range(HG):
                            dve.wait_ge(s_done, H * sb_ + HG * sg + j + 1)
                            v.tensor_reduce(mx[:, :, j], S[j % 2][:, :].rearrange("p (c t) -> p c t", c=TC), AX.X,
                                            ALU.max, negate=True).then_inc(max_done, 1)
                        dve.wait_ge(max_done, H * sb_ + HG * (sg + 1))
                        wait(dve, mT_done, G * sb_ + sg)
                        link = Chain(dve, msplit, G * sb_ + sg, 2)
                        link(v.tensor_copy(mm[:, :, 0:HG], mx[:, :, :]))
                        v.tensor_tensor(mm[:, :, HG:2 * HG], mx[:, :, :], mm[:, :, 0:HG].bitcast(F32), ALU.subtract).then_inc(msplit, 1)
                    if g < KC and st.next:
                        dve.wait_ge(qk_high, KC * b + g + 1)
                        for n in range(2):
                            last = v.scalar_tensor_tensor(part[:, 2 * n + 1, :], M[0][:, n * T:(n + 1) * T], bqk[:, n, g:g + 1],
                                                          part[:, 2 * n, :].bitcast(F32), ALU.add, ALU.subtract)
                        last.then_inc(qk_low, 1)
                    if g == 3 and st.next:
                        dve.wait_ge(v_proj, b + 1)
                        wait(dve, pv_done, G * b)
                        for c in range(TC):
                            last = v.tensor_tensor(va[:, c, :, 0:D], M[0][:, c * C:(c + 1) * C].rearrange("p (h d) -> p h d", d=D),
                                                   bv_all[:, :].rearrange("p (h d) -> p h d", d=D), ALU.add)
                        last.then_inc(v_ready, 1)
                    if g % 2 and st.cur:
                        wait_apart(dve, (pv_done, G * i + g + 1), (o_done, i))
                        pair = on[:, g - 1:g + 1, :].rearrange("p g t -> p (g t)")
                        v.stream_shuffle(pair, PV[g // 2][:, :], [r + D if r < D else r for r in range(HR)]).then_inc(den_ready, 1)
                        dve.wait_ge(den_ready, 4 * i + g)
                        v.reciprocal(pair, pair).then_inc(den_ready, 1)
                        dve.wait_ge(den_ready, 4 * i + g + 1)
                        v.tensor_tensor(pair, PV[g // 2][:, :], pair, ALU.mult).then_inc(norm_done, 1)
                    if g == 1 and st.gate:
                        dve.wait_ge(lg_copied, i - 1)
                        c0 = ds((i - 2) * TC, TC) if not isinstance(i, int) else slice((i - 2) * TC, (i - 1) * TC)
                        wait(dve, rows_sent, 64 * (i - 2))
                        link = Chain(dve, choice, i - 2, CHOICE_STEPS)
                        v.tensor_copy(logits[:, c0, :], lg[:, :, :])
                        for c in range(TC):
                            last = v.max(lg8[:, c, :], lg[:, c, :])
                        link(last, wait_apart)
                        for c in range(TC):
                            last = v.max_index(ix8[:, c, :], lg8[:, c, :], lg[:, c, :])
                        link(last)
                        for k in range(2):
                            last = v.tensor_tensor(pick[:, k, :, :], iota_e[:, :].unsqueeze(1).to_broadcast([P, TC, E]),
                                                   ix8[:, :, k:k + 1].to_broadcast([P, TC, E]), ALU.is_equal)
                        link(last)
                        v.tensor_copy(picked[:, :, c0], ix8[:, :, 0:2].rearrange("p c k -> p k c"))
                        v.tensor_copy(x2[:, :, C], token[:, :])
                        link(v.tensor_tensor(mask[:, :, :], pick[:, 0], pick[:, 1], ALU.add))
                        link(v.tensor_copy(x2[:, :, C + 1], ix8[:, :, 0]))
                        link(v.tensor_scalar(token[:, :], token[:, :], float(T), None, ALU.add))
                    if g == 1 and st.post:
                        dve.wait_ge(o_done, i)
                        dve.wait_ge(x_loaded, 16 * i)
                        flat = x1[:, :, :].rearrange("p c n -> p (c n)")
                        v.tensor_tensor(flat, M[1][:, :], flat, ALU.add).then_inc(z1_done, 1)
                        dve.wait_ge(z1_done, i)
                        norm_stats(ln1_stats, i - 1, x1, 0)
                    if g == 2 and st.gate:
                        dve.wait_ge(cum_copied, i - 1)
                        link = Chain(dve, seat_chain, i - 2, SEAT_STEPS)
                        link(v.tensor_tensor(seat[:, :, :], cum[:, 0:TC, :], count[:, :].unsqueeze(1).to_broadcast([P, TC, E]), ALU.add))
                        link(v.tensor_tensor(count[:, :], cum[:, TC, :], count[:, :], ALU.add))
                        for k in range(2):
                            last = v.tensor_tensor(pick[:, k], pick[:, k], seat[:, :, :], ALU.mult)
                        link(last)
                        link(v.tensor_reduce(seat_k[:, :, :], pick[:, :, :, :], AX.X, ALU.add))
                        wait(dve, rows_sent, 64 * (i - 2))
                        link(v.tensor_copy(seat_i[:, :, :], seat_k[:, :, :]))
                    if g == 3 and st.post:
                        dve.wait_ge(xo_done, i)
                        flat = x1[:, :, :].rearrange("p c n -> p (c n)")
                        v.scalar_tensor_tensor(flat, M[1][:, :], 0.5, flat, ALU.mult, ALU.add).then_inc(z2_done, 1)
                        dve.wait_ge(z2_done, i)
                        norm_stats(ln2_stats, i - 1, x1, 1)
            pipeline(dve, body)

            dve.wait_ge(post_const, 2)
            link = Chain(dve, table, 0, TABLE_STEPS)
            link(v.scalar_tensor_tensor(num[:, :], iota_e[:, :], -float(CAP), count[:, :], ALU.mult, ALU.add))
            link(v.tensor_tensor(over[:, :, :], num[:, :].unsqueeze(2).to_broadcast([P, E, N // ET]),
                                 fulls[:, :].unsqueeze(1).to_broadcast([P, E, N // ET]), ALU.is_gt))
            link(v.tensor_reduce(tiles_of[:, :], over[:, :, :], AX.X, ALU.add))
            link(v.tensor_tensor_scan(last_of[:, :], ones_e[:, :], tiles_of[:, :], 0.0, ALU.mult, ALU.add))
            link(v.tensor_tensor(base_of[:, :], tiles_of[:, :], last_of[:, :], ALU.subtract))
            link(v.tensor_scalar(base_of[:, :], base_of[:, :], float(ET), None, ALU.mult))
            link(v.scalar_tensor_tensor(base_of[:, :], iota_e[:, :], float(CAP), base_of[:, :], ALU.mult, ALU.add))
            link(v.tensor_scalar(num[:, 0:1], last_of[:, E - 1:E], -1.0, None, ALU.add))
            link(v.tensor_scalar(tau[:, :], tau[:, :], num[:, 0:1], None, ALU.min))
            link(v.tensor_tensor(by_e[:, :, :], last_of[:, :].unsqueeze(1).to_broadcast([P, TILES, E]),
                                 tau[:, :].unsqueeze(2).to_broadcast([P, TILES, E]), ALU.is_le))
            link(v.tensor_reduce(tile_e[:, :], by_e[:, :, :], AX.X, ALU.add))
            v.tensor_copy(tab[:, 0, :], tile_e[:, :])
            link(v.tensor_tensor(by_e[:, :, :], iota_e[:, :].unsqueeze(1).to_broadcast([P, TILES, E]),
                                 tile_e[:, :].unsqueeze(2).to_broadcast([P, TILES, E]), ALU.is_equal))
            v.tensor_copy(cnt_i[:, :], count[:, :])
            v.tensor_tensor(by_e[:, :, :], by_e[:, :, :], base_of[:, :].unsqueeze(1).to_broadcast([P, TILES, E]),
                            ALU.mult).then_inc(gating, 1)
            dve.wait_ge(gating, 1)
            link(v.tensor_reduce(tile_row[:, :], by_e[:, :, :], AX.X, ALU.add))
            link(v.scalar_tensor_tensor(tab[:, 1, :], tau[:, :], float(ET), tile_row[:, :], ALU.mult, ALU.add))
            link.end()

            def spread(t):
                return t.unsqueeze(2).to_broadcast([P, NT, E])

            def gating_weights():
                n = [1]

                def link(ins):
                    n[0] += 1
                    ins.then_inc(gating, 1)
                    dve.wait_ge(gating, n[0])
                for k in range(2):
                    v.tensor_tensor(chosen[:, k], iota_e[:, :].unsqueeze(1).to_broadcast([P, NT, E]), spread(picked[:, k, :]), ALU.is_equal)
                link(v.tensor_reduce(gmax[:, :], logits[:, :, :], AX.X, ALU.max))
                link(v.tensor_tensor(gate[:, :, :], logits[:, :, :], spread(gmax[:, :]), ALU.subtract))
                dve.wait_ge(gate_exp, 1)
                link(v.tensor_reduce(gsum[:, :], gate[:, :, :], AX.X, ALU.add))
                link(v.reciprocal(gsum[:, :], gsum[:, :]))
                link(v.tensor_tensor(gate[:, :, :], gate[:, :, :], spread(gsum[:, :]), ALU.mult))
                for k in range(2):
                    last = v.tensor_tensor(gprod[:, k, :, :], chosen[:, k, :, :], gate[:, :, :], ALU.mult)
                link(last)
                link(v.tensor_reduce(weight[:, :, :], gprod[:, :, :, :], AX.X, ALU.add))
                link(v.scalar_tensor_tensor(gsum[:, :], weight[:, 0, :], 1e-9, weight[:, 1, :], ALU.add, ALU.add))
                link(v.reciprocal(gsum[:, :], gsum[:, :]))
                for k in range(2):
                    last = v.tensor_tensor(gprod[:, k, :, :], chosen[:, k, :, :], yscale[:, :].unsqueeze(1).to_broadcast([P, NT, E]), ALU.mult)
                link(last)
                link(v.tensor_reduce(gscale[:, :, :], gprod[:, :, :, :], AX.X, ALU.add))
                link(v.tensor_tensor(weight[:, :, :], weight[:, :, :], gsum[:, :].unsqueeze(1).to_broadcast([P, 2, NT]), ALU.mult))
                link(v.tensor_tensor(weight[:, :, :], weight[:, :, :], gscale[:, :, :], ALU.mult))
            gating_weights()

            def turn(t):
                dve.wait_ge(xs_high_done, t + 1)
                v.scalar_tensor_tensor(xs[1][:, :, :].rearrange("p k t -> p (k t)"), XB[:, :], XS,
                                       xs[0][:, :, :].rearrange("p k t -> p (k t)"), ALU.mult, ALU.subtract).then_inc(xs_low_done, 1)

            def halves(t):
                dve.wait_ge(tile_loaded, 16 * (t + 1))
                wait(dve, dest_ready, t)
                link = Chain(dve, meta_chain, t, 2)
                link(v.tensor_copy(meta_next[:, :, :], xt[:, :, C:ROW]))
                e_col = tile_e[:, t:t + 1] if isinstance(t, int) else tile_e[:, ds(t, 1)]
                link(v.tensor_scalar(other[:, :], meta_next[:, :, 1], e_col, float(N), ALU.not_equal, ALU.mult))

            def tile(t, more):
                halves(t)
                for q in range(FC // 2):
                    dve.wait_ge(hid_high, FC // 2 * t + q + 1)
                    v.scalar_tensor_tensor(hs[1][:, 2 * q:2 * q + 2, :].rearrange("p f t -> p (f t)"), HB[q][:, :], 0.0,
                                           hs[0][:, 2 * q:2 * q + 2, :].rearrange("p f t -> p (f t)"),
                                           ALU.max, ALU.subtract).then_inc(hid_low, 1)
                wait(dve, y_sent, 16 * ETC * t)
                v.tensor_tensor(dest[:, :], other[:, :], meta_next[:, :, 0], ALU.add).then_inc(dest_ready, 1)
                if more:
                    turn(t + 1)
            turn(0)
            tile(0, True)
            with dve.Fori(0, TILES - 2, 1) as t:
                tile(t + 1, True)
            tile(TILES - 1, False)

            def fin(n, q):
                dve.wait_ge(fin_loaded[q], 32 * (n + 1))
                link = Chain(dve, fin_chain, 2 * n + q, FIN_STEPS)
                for k in range(2):
                    for c in range(TC):
                        z = row_of(fx, 2 * (2 * n + q) + c)
                        w_col = weight[:, k, ds(2 * (2 * n + q) + c, 1)]
                        last = v.scalar_tensor_tensor(z, fy[q][:, k, c, :], w_col, z, ALU.mult, ALU.add)
                    link(last, wait_apart)
                for c in range(TC):
                    last = v.bn_stats(fbn[:, q, c, :], row_of(fx, 2 * (2 * n + q) + c))
                link(last, wait_apart)
                for c in range(TC):
                    last = v.bn_aggr(fmv[:, q, c, :], fbn[:, q, c, :])
                link(last)
                scale_and_shift(link, fmv[:, q], frs[:, q], froot[:, q])
                link.end()
            dve.wait_ge(fx_loaded, 16)
            with dve.Fori(0, NB // 2, 1) as n:
                for q in range(2):
                    fin(n, q)

        @block.tensor
        def _(pe):
            mmul = nc.tensor.matmul
            pe.wait_ge(lora_loaded, 16 * 14)
            pe.wait_ge(wo_loaded, 16 * 6)
            for n in range(3):
                for k in range(KC):
                    last = mmul((S[0], S[1], ST[0])[n][:, k * C:(k + 1) * C], lora_a[:, n, k * P:(k + 1) * P], lora_b[:, n, :],
                                start=True, stop=True)
                last.then_inc(lora_done, 1)
            for g in range(G):
                last = mmul((ST[1], PV[0])[g // 2][:, g % 2 * C:(g % 2 + 1) * C], lora_ao[:, g, :], lora_b[:, 3, :],
                            start=True, stop=True)
            last.then_inc(lora_done, 1)
            pe.wait_ge(const_ready, 2)
            for e in range(E):
                pe.wait_ge(absmax_done, e + 1)
                nc.tensor.transpose(M[0][0:2, 0:P], absmax[:, :], ident[:, :]).then_inc(absmax_turned, 1)
                pe.wait_ge(diag_done, e + 1)
                mmul(M[1][:, 0:2], ones_2[:, :], diag[:, :], start=True, stop=True).then_inc(peak_spread, 1)

            def mixing_bank_free(i, g):
                if g == 0:
                    wait(pe, z2_done, min_of(i - 1))
                elif g == 1:
                    wait(pe, x2T_copied, min_of(i - 1))
                elif g == 2:
                    wait(pe, z1_done, min_of(i))
                else:
                    wait(pe, h_copied, min_of(i))
                    wait(pe, cum_copied, min_of(i - 1))

            def body(i, st):
                b = i + 1
                for g in range(G):
                    sb_, sg, s_on = scored(i, g, st)
                    if st.cur:
                        pe.wait_ge(mrow_set[g], 16 * (i + 1))
                    for j in range(HG):
                        if st.cur:
                            wait(pe, exp_done, H * i + HG * g + j - 1)
                            for c in range(TC):
                                last = mmul(ST[j % 2][:, c * T:(c + 1) * T], ks[0:KROWS, g, j, c * P:(c + 1) * P],
                                            qs[0:KROWS, g, j, :], start=True, stop=True)
                            last.then_inc(st_done, 1)
                        if s_on and g < 3:
                            score(sb_, sg, j)
                    if g == 3 and s_on and st.cur:
                        for j in range(HG):
                            score(sb_, sg, j)
                    if g < KC and st.next:
                        pe.wait_ge(xT_loaded, 16 * (b + 1))
                        wait(pe, v_ready if g == 0 else qk_low, b if g == 0 else 2 * b + 1)
                        for n, w in enumerate((wq, wk)):
                            for k in range(KC):
                                last = mmul(M[0][:, n * T:(n + 1) * T], w[:, k, g * P:(g + 1) * P], xT_sb[:, k, :],
                                            start=k == 0, stop=k == KC - 1)
                        last.then_inc(qk_proj, 1)
                    if g == 2 and st.post:
                        pe.wait_ge(x1_ready, i)
                        if st.next:
                            pe.wait_ge(qk_low, KC * (b + 1))
                        else:
                            pe.wait_ge(x1T_copied, i - 1)
                        for k in range(KC):
                            for c in range(TC):
                                last = nc.tensor.transpose(M[0][:, k * T + c * P:k * T + (c + 1) * P], x1[:, c, k * P:(k + 1) * P], ident[:, :])
                        last.then_inc(x1T_done, 1)
                    if g == 3 and st.next:
                        if st.post:
                            pe.wait_ge(x1T_copied, i)
                        else:
                            pe.wait_ge(qk_low, KC * (b + 1))
                        for c in range(TC):
                            for k in range(KC):
                                last = mmul(M[0][:, c * C:(c + 1) * C], xT_sb[:, k, c * P:(c + 1) * P], wv[:, k, :],
                                            start=k == 0, stop=k == KC - 1)
                        last.then_inc(v_proj, 1)
                    if g == 3 and s_on and not st.cur:
                        for j in range(HG):
                            score(sb_, sg, j)
                    mixing_bank_free(i, g)
                    if g == 1 and st.gate:
                        pe.wait_ge(x2T_copied, i - 1)
                        for c in range(TC):
                            for k in range(KC):
                                last = mmul(M[1][:, T + c * E:T + (c + 1) * E], x2T[:, k, c * P:(c + 1) * P], wg[:, k, :],
                                            start=k == 0, stop=k == KC - 1)
                        last.then_inc(lg_done, 1)
                    if s_on:
                        pe.wait_ge(msplit, 2 * (G * sb_ + sg + 1))
                        wait(pe, mT_copied, G * sb_ + sg)
                        for c in range(TC):
                            last = nc.tensor.transpose(M[1][0:2 * HG, c * P:(c + 1) * P], mm[:, c, :].bitcast(F32), ident[:, :])
                        last.then_inc(mT_done, 1)
                    if st.cur:
                        pe.wait_ge(exp_done, H * i + HG * (g + 1))
                        pe.wait_ge(v_ready, i + 1)
                        if g % 2 == 0:
                            wait(pe, norm_done, 2 * i + g // 2 - 1)
                        for c in range(TC):
                            for j in range(HG):
                                last = mmul(PV[g // 2][j * HR:(j + 1) * HR, g % 2 * T:(g % 2 + 1) * T], va[:, c, g * HG + j, :],
                                            pt[:, j, c * T:(c + 1) * T], start=c == 0, stop=c == TC - 1)
                        last.then_inc(pv_done, 1)
                    if s_on:
                        pe.wait_ge(mT_copied, G * sb_ + sg + 1)
                    if g == 0 and st.gate:
                        pe.wait_ge(x2_ready, i - 1)
                        for k in range(KC):
                            for c in range(TC):
                                last = nc.tensor.transpose(M[1][:, k * T + c * P:k * T + (c + 1) * P], x2[:, c, k * P:(k + 1) * P], ident[:, :])
                        last.then_inc(x2T_done, 1)
                    if g == 1 and st.post:
                        pe.wait_ge(norm_done, 2 * i)
                        wait(pe, lg_copied, min_of(i - 1))
                        for c in range(TC):
                            for gg in range(G):
                                last = mmul(M[1][:, c * C:(c + 1) * C], on[:, gg, c * P:(c + 1) * P], wo[:, gg, :],
                                            start=gg == 0, stop=gg == G - 1)
                        last.then_inc(o_done, 1)
                    if g == 2 and (st.post or st.gate):
                        if st.gate:
                            pe.wait_ge(choice, CHOICE_STEPS * (i - 1))
                            sums = M[1][:, CUM:CUM + 3 * E].rearrange("p (c e) -> p c e", e=E)
                            mmul(sums[:, 0, :], before[:, :], mask[:, 0, :], start=True, stop=True)
                            mmul(sums[:, 1, :], before[:, :], mask[:, 1, :], start=True, stop=False)
                            mmul(sums[:, 1, :], ones_sq[:, :], mask[:, 0, :], start=False, stop=True)
                            mmul(sums[:, 2, :], ones_sq[:, :], mask[:, 0, :], start=True, stop=False)
                            last = mmul(sums[:, 2, :], ones_sq[:, :], mask[:, 1, :], start=False, stop=True)
                        if st.post:
                            pe.wait_ge(x1T_copied, i)
                            pe.wait_ge(cT_loaded, 16 * i)
                            for k in range(KC):
                                last = mmul(M[1][0:S2, 0:T], cT[:, k, :], x1T[:, k, :], start=k == 0, stop=k == KC - 1)
                        last.then_inc(mid_done, 1)
                    if g == 3 and st.post:
                        pe.wait_ge(gelu_out, 2 * i)
                        pe.wait_ge(cr_loaded, 16 * i)
                        for c in range(TC):
                            last = mmul(M[1][:, c * C:(c + 1) * C], hv[:, c * P:(c + 1) * P], cr[:, :], start=True, stop=True)
                        last.then_inc(xo_done, 1)

            def score(sb_, sg, j):
                if j == 0:
                    pe.wait_ge(slot_loaded[sg], 64 * (sb_ + 1))
                    pe.wait_ge(mrow_zero, G * sb_ + sg + 1)
                wait(pe, max_done, H * sb_ + HG * sg + j - 1)
                for c in range(TC):
                    last = mmul(S[j % 2][:, c * T:(c + 1) * T], qs[0:KROWS, sg, j, c * P:(c + 1) * P],
                                ks[0:KROWS, sg, j, :], start=True, stop=True)
                last.then_inc(s_done, 1)
            pe.wait_ge(rows_const, 2)
            pe.wait_ge(fold_done, FOLDS)
            pe.wait_ge(scale_done, E + 1)
            pipeline(pe, body)

            pe.wait_ge(low_done, 2 * E)
            pe.wait_ge(high_done, 2 * E)

            def turn(t):
                pe.wait_ge(tile_loaded, 16 * (t + 1))
                wait(pe, xs_low_done, t)
                for k in range(KC):
                    for c in range(ETC):
                        last = nc.tensor.transpose(XB[:, k * ET + c * P:k * ET + (c + 1) * P], xt[:, c, k * P:(k + 1) * P], ident[:, :])
                last.then_inc(turned, 1)

            def tile(t, more):
                e = pe.value_load(tab[0:1, 0, t:t + 1] if isinstance(t, int) else tab[0:1, 0, ds(t, 1)], min_val=0, max_val=E - 1)
                pe.wait_ge(xs_low_done, t + 1)
                for q in range(FC // 2):
                    for f in (2 * q, 2 * q + 1):
                        n = 0
                        for k in range(KC):
                            for w, xp in ((w_high[0], xs[0]), (w_high[0], xs[1]), (w_low[0], xs[0])):
                                last = mmul(HB[q][:, f % 2 * ET:(f % 2 + 1) * ET],
                                            w[:, ds(e, 1), k * F + f * P:k * F + (f + 1) * P].rearrange("p a f -> p (a f)"),
                                            xp[:, k, :], start=n == 0, stop=n == 3 * KC - 1)
                                n += 1
                    last.then_inc(up_done, 1)
                if more:
                    turn(t + 1)
                wait(pe, y_copied, t)
                for f in range(FC):
                    if f % 2 == 0:
                        pe.wait_ge(hid_low, FC // 2 * t + f // 2 + 1)
                    for c in range(ETC):
                        for n, (w, hp) in enumerate(((w_high[1], hs[0]), (w_high[1], hs[1]), (w_low[1], hs[0]))):
                            last = mmul(YB[c][:, 0:C], hp[:, f, c * P:(c + 1) * P],
                                        w[:, ds(e, 1), f * C:(f + 1) * C].rearrange("p a f -> p (a f)"),
                                        start=f == 0 and n == 0, stop=f == FC - 1 and n == 2)
                last.then_inc(down_done, 1)
            turn(0)
            tile(0, True)
            with pe.Fori(0, TILES - 2, 1) as t:
                tile(t + 1, True)
            tile(TILES - 1, False)


def kernel(x, ctx_1024, L0_attn_Wq, L0_attn_bq, L0_attn_Aq, L0_attn_Bq, L0_attn_Wk, L0_attn_bk, L0_attn_Ak,
           L0_attn_Bk, L0_attn_Wv, L0_attn_bv, L0_attn_Av, L0_attn_Bv, L0_attn_Wo, L0_attn_bo, L0_attn_Ao,
           L0_attn_Bo, L0_ffn_Wg, L0_ffn_W1, L0_ffn_W2):
    import numpy as np
    import concourse.bacc as bacc
    from concourse.bass_utils import run_bass_kernel_spmd

    def turned(a):
        return np.ascontiguousarray(np.swapaxes(np.asarray(a), -1, -2))

    def columns(a):
        return turned(np.asarray(a).reshape(-1, 128))

    arrays = {
        "x": np.asarray(x), "xT": turned(x), "ctx": np.asarray(ctx_1024), "ctxT": turned(ctx_1024),
        "WqT": turned(L0_attn_Wq), "WkT": turned(L0_attn_Wk), "WvT": turned(L0_attn_Wv), "WoT": turned(L0_attn_Wo),
        "Aq": np.asarray(L0_attn_Aq), "Ak": np.asarray(L0_attn_Ak), "Av": np.asarray(L0_attn_Av), "Ao": np.asarray(L0_attn_Ao),
        "BqT": turned(L0_attn_Bq), "BkT": turned(L0_attn_Bk), "BvT": turned(L0_attn_Bv), "BoT": turned(L0_attn_Bo),
        "bq": columns(L0_attn_bq), "bk": columns(L0_attn_bk), "bv": np.asarray(L0_attn_bv), "bo": np.asarray(L0_attn_bo),
        "Wg": np.asarray(L0_ffn_Wg), "W1": np.asarray(L0_ffn_W1), "W2": np.asarray(L0_ffn_W2),
    }
    arrays = {"in_" + k: np.ascontiguousarray(a) for k, a in arrays.items()}
    nc = bacc.Bacc("TRN2", target_bir_lowering=False, num_devices=1)
    args = [nc.dram_tensor(k, a.shape, mybir.dt.from_np(a.dtype), kind="ExternalInput").ap() for k, a in arrays.items()]
    out = nc.dram_tensor("out", x.shape, mybir.dt.float32, kind="ExternalOutput").ap()
    decoder_layer(nc, *args, out)
    result = run_bass_kernel_spmd(nc, [arrays], core_ids=[0])
    return result.results[0]["out"]
```

```python
import concourse.bass as bass
from concourse import mybir
from contextlib import ExitStack


class Chain:

    def __init__(self, eng, sem, piece, steps):
        self.eng, self.sem, self.base, self.steps, self.n = eng, sem, piece * steps, steps, 0

    def __call__(self, ins, wait=None):
        self.n += 1
        assert self.n <= self.steps
        ins.then_inc(self.sem, 1)
        if wait:
            wait(self.eng, (self.sem, self.base + self.n))
        else:
            self.eng.wait_ge(self.sem, self.base + self.n)

    def end(self):
        assert self.n == self.steps, (self.n, self.steps)


class Stages:

    def __init__(self, i, batches):
        self.next = 0 <= i + 1 < batches
        self.cur = 0 <= i < batches
        self.post = 0 <= i - 1 < batches
        self.cross = 0 <= i - 2 < batches
        self.send = 0 <= i - 3 < batches


def decoder_layer(nc, x, xT, ctx, ctxT, WqT, WkT, WvT, WoT, Aq, Ak, Av, Ao, BqT, BkT, BvT, BoT,
                  bq, bk, bv, bo, Wg, W1, W2, out):
    F32, F32R, F16 = mybir.dt.float32, mybir.dt.float32r, mybir.dt.float16
    I32, U32 = mybir.dt.int32, mybir.dt.uint32
    ALU, ACT, AX = mybir.AluOpType, mybir.ActivationFunctionType, mybir.AxisListType
    ds = bass.ds

    P = 128
    NB, T, C = x.shape
    S2 = ctx.shape[1]
    R = Aq.shape[0]
    LORA = 2.0
    D = 16
    H = C // D
    KC, TC = C // P, T // P
    HG = 4
    G = H // HG
    HR = P // HG
    MROW = 4 * D
    KROWS = MROW + 2
    E, F = W1.shape[0], W1.shape[2]
    FC = F // P
    N = NB * T
    NT = N // P
    ET = 256
    ETC = ET // P
    CAP = N + ET
    TILES = (2 * N + E * (ET - 1)) // ET
    ROW = C + 2
    DROP = 2 * N
    EPS = 1e-5
    XS, WS = 4.0, 16.0
    EXP_MASK, EXP_ONE = 0x7F800000, 1 << 23
    CUM = 288
    GELU_LEAST = -50.0
    GELU_A, GELU_C = 0.044715, 0.7978845608028654

    x_tok = x.rearrange("b (c p) n -> b p c n", p=P)
    x_ch = xT.rearrange("b (k p) t -> b p k t", p=P)
    ctx_ch = ctxT.rearrange("b (k p) t -> b p k t", p=P)
    w1_e = W1.rearrange("e (k p) f -> e p k f", p=P)
    w2_e = W2.rearrange("e (c p) n -> e p c n", p=P)

    q_parts = nc.dram_tensor("q_parts", [H, 3, D, T], F32, kind="Internal").ap()
    k_parts = nc.dram_tensor("k_parts", [H, 2, D, T], F32, kind="Internal").ap()
    x2_rows = nc.dram_tensor("x2_rows", [N, C], F32, kind="Internal").ap()
    sent = nc.dram_tensor("sent", [E * CAP, ROW], F32, kind="Internal").ap()
    mixed = nc.dram_tensor("mixed", [2 * N, C], F32, kind="Internal").ap()
    q_rows = q_parts.rearrange("h s d t -> (s d) h t")
    k_rows = k_parts.rearrange("h s d t -> (s d) h t")

    es = ExitStack()
    with es:
        def sem(name):
            return es.enter_context(nc.semaphore(name))

        def pb(name):
            return es.enter_context(nc.psum_tensor(name, [P, 512], F32))

        top = [(nc.sbuf_base + 63) // 64 * 64]

        def sb(name, shape, dt):
            width = 2 if dt == F16 else 4
            for s in shape[1:]:
                width *= s
            t = nc.alloc_sbuf_tensor_at(name, shape, dt, offset=top[0])
            top[0] += (width + 31) // 32 * 32
            assert top[0] <= nc.sbuf_usable_end, (name, top[0])
            return t

        w_high = [sb("w1_high", [P, E, KC * F], F16), sb("w2_high", [P, E, FC * C], F16)]
        w_low = [sb("w1_low", [P, E, KC * F], F16), sb("w2_low", [P, E, FC * C], F16)]
        ident = sb("ident", [P, P], F32)
        ones_sq = sb("ones_sq", [P, P], F16)
        before = sb("before", [P, P], F16)
        iota_e = sb("iota_e", [P, E], F32)
        yscale = sb("yscale", [P, E], F32)
        count = sb("count", [P, E], F32)
        logits = sb("logits", [P, NT, E], F32)
        picked = sb("picked", [P, 2, NT], F32)
        weight = sb("weight", [P, 2, NT], F32)
        token = sb("token", [P, TC], F32)
        eps_col = sb("eps_col", [P, 1], F32)
        one_col = sb("one_col", [P, 1], F32)
        phase = top[0]
        STAGES = 3

        wq = sb("wq", [P, KC, C], F32)
        wk = sb("wk", [P, KC, C], F32)
        wv = sb("wv", [P, KC, C], F32)
        wo = sb("wo", [P, G, C], F32)
        bqk = sb("bqk", [P, 2, KC], F32)
        bv_all = sb("bv_all", [P, C], F32)
        wg = sb("wg", [P, KC, E], F32)
        staging = top[0]
        xT_sb = sb("xT_sb", [P, KC, T], F32)
        x_sb = sb("x_sb", [P, TC, C], F32)
        part = sb("part", [P, 4, T], F32R)
        qs = sb("qs", [P, G, HG, T], F32R)
        ks = sb("ks", [P, G, HG, T], F32R)
        pt = sb("pt", [P, HG, TC * T], F32)
        va = sb("va", [P, TC, H, HR], F32)
        mx = sb("mx", [P, TC, HG], F32)
        mm = sb("mm", [P, TC, 2 * HG], F32R)
        mT = sb("mT", [2 * HG, T], F32)
        on = sb("on", [P, G, T], F32)
        x1 = sb("x1", [P, TC, C], F32)
        x1T = sb("x1T", [P, KC, T], F32)
        x2T, hv, hu = x1T, x1T[0:S2, 0, :], x1T[0:S2, 1, :]
        cT = sb("cT", [P, KC, S2], F32)
        cr = sb("cr", [S2, C], F32)
        x2 = sb("x2", [P, TC, ROW], F32)
        bn = sb("bn", [P, 2, TC, 6], F32)
        mv = sb("mv", [P, 2, TC, 2], F32)
        rstd = sb("rstd", [P, 2, TC, 2], F32)
        lnv = sb("lnv", [P, 2, TC, 1], F32)
        neg = sb("neg", [P, 2, TC, 1], F32)
        lg = sb("lg", [P, TC, E], F32)
        lg8 = sb("lg8", [P, TC, 8], F32)
        ix8 = sb("ix8", [P, TC, 8], U32)
        pick = sb("pick", [P, 2, TC, E], F32)
        mask = sb("mask", [P, TC, E], F16)
        cum = sb("cum", [P, TC + 1, E], F32)
        seat = sb("seat", [P, TC, E], F32)
        seat_k = sb("seat_k", [P, 2, TC], F32)
        seat_i = sb("seat_i", [P, 2, TC], I32)

        top[0] = staging
        stage = [sb(f"stage{i}", [P, 2, KC * F], F32) for i in range(STAGES)]
        lora_a = sb("lora_a", [R, 3, C], F32)
        lora_ao = sb("lora_ao", [R, G, P], F32)
        lora_b = sb("lora_b", [R, 4, C], F32)
        absmax = sb("absmax", [P, 2], F32)
        peak = sb("peak", [2, 1], F32)
        diag = sb("diag", [2, 2], F32)
        ones_2 = sb("ones_2", [2, P], F32)
        wpow = sb("wpow", [P, 2 * E], F32)
        winv = sb("winv", [P, 2 * E], F32)

        top[0] = phase
        xt = sb("xt", [P, ETC, ROW], F32)
        xs = [sb(n, [P, KC, ET], F16) for n in ("xs_high", "xs_low")]
        hs = [sb(n, [P, FC, ET], F16) for n in ("hs_high", "hs_low")]
        ys = sb("ys", [P, ETC, C], F32)
        meta_next = sb("meta_next", [P, ETC, 2], F32)
        other = sb("other", [P, ETC], F32)
        dest = sb("dest", [P, ETC], I32)
        fx = sb("fx", [P, NT, C], F32)
        fy = [sb(f"fy{i}", [P, 2, TC, C], F32) for i in range(2)]
        fo = [sb(f"fo{i}", [P, TC, C], F32) for i in range(2)]
        fbn = sb("fbn", [P, 2, TC, 6], F32)
        fmv = sb("fmv", [P, 2, TC, 2], F32)
        frs = sb("frs", [P, 2, TC, 2], F32)
        flnv = sb("flnv", [P, 2, TC, 1], F32)
        fneg = sb("fneg", [P, 2, TC, 1], F32)
        pad = sb("pad", [P, ETC, ROW], F32)
        fulls = sb("fulls", [P, FC * 2], F32)
        over = sb("over", [P, E, FC * 2], F32)
        num = sb("num", [P, E], F32)
        tiles_of = sb("tiles_of", [P, E], F32)
        last_of = sb("last_of", [P, E], F32)
        base_of = sb("base_of", [P, E], F32)
        ones_e = sb("ones_e", [P, E], F32)
        tau = sb("tau", [P, TILES], F32)
        by_e = sb("by_e", [P, TILES, E], F32)
        tile_e = sb("tile_e", [P, TILES], F32)
        tile_row = sb("tile_row", [P, TILES], F32)
        tab = sb("tab", [P, 2, TILES], I32)
        cnt_i = sb("cnt_i", [P, E], I32)
        chosen = sb("chosen", [P, 2, NT, E], F32)
        gmax = sb("gmax", [P, NT], F32)
        gate = sb("gate", [P, NT, E], F32)
        gprod = sb("gprod", [P, 2, NT, E], F32)
        gscale = sb("gscale", [P, 2, NT], F32)
        gsum = sb("gsum", [P, NT], F32)
        assert N // ET == FC * 2

        S = [pb(f"S{i}") for i in range(2)]
        ST = [pb(f"ST{i}") for i in range(2)]
        PV = [pb(f"PV{i}") for i in range(2)]
        M = [pb(f"M{i}") for i in range(2)]
        HB = [S[0], S[1], ST[0], ST[1]]
        YB, XB = PV, M[0]

        pool_consts = sem("pool_consts")
        const_ready = sem("const_ready")
        lora_loaded = sem("lora_loaded")
        wo_loaded = sem("wo_loaded")
        lora_done = sem("lora_done")
        fold_chain = sem("fold_chain")
        fold_done = sem("fold_done")
        stage_loaded = [sem(f"stage_loaded{i}") for i in range(STAGES)]
        absmax_done = sem("absmax_done")
        absmax_turned = sem("absmax_turned")
        diag_chain = sem("diag_chain")
        diag_done = sem("diag_done")
        peak_spread = sem("peak_spread")
        scale_chain = sem("scale_chain")
        scale_done = sem("scale_done")
        high_done = sem("high_done")
        low_done = sem("low_done")
        rows_const = sem("rows_const")
        xT_loaded = sem("xT_loaded")
        x_loaded = sem("x_loaded")
        cT_loaded = sem("cT_loaded")
        cr_loaded = sem("cr_loaded")
        qk_proj = sem("qk_proj")
        qk_high = sem("qk_high")
        qk_low = sem("qk_low")
        part_sent = [sem(f"part_sent{m}") for m in range(KC)]
        slot_loaded = [sem(f"slot_loaded{g}") for g in range(G)]
        mrow_zero = sem("mrow_zero")
        mrow_set = [sem(f"mrow_set{g}") for g in range(G)]
        v_proj = sem("v_proj")
        v_ready = sem("v_ready")
        s_done = sem("s_done")
        max_done = sem("max_done")
        msplit = sem("msplit")
        mT_done = sem("mT_done")
        mT_copied = sem("mT_copied")
        st_done = sem("st_done")
        exp_done = sem("exp_done")
        pv_done = sem("pv_done")
        den_ready = sem("den_ready")
        den_log = sem("den_log")
        den_inverse = sem("den_inverse")
        norm_done = sem("norm_done")
        o_done = sem("o_done")
        z1_done = sem("z1_done")
        ln1_stats = sem("ln1_stats")
        ln1_scale = sem("ln1_scale")
        x1_ready = sem("x1_ready")
        x1T_done = sem("x1T_done")
        x1T_copied = sem("x1T_copied")
        h_done = sem("h_done")
        h_copied = sem("h_copied")
        gelu_in = sem("gelu_in")
        sigmoid = sem("sigmoid")
        gelu_out = sem("gelu_out")
        xo_done = sem("xo_done")
        z2_done = sem("z2_done")
        ln2_stats = sem("ln2_stats")
        ln2_scale = sem("ln2_scale")
        x2_ready = sem("x2_ready")
        x2T_done = sem("x2T_done")
        x2T_copied = sem("x2T_copied")
        x2_stored = sem("x2_stored")
        lg_done = sem("lg_done")
        lg_copied = sem("lg_copied")
        choice = sem("choice")
        cum_copied = sem("cum_copied")
        seat_chain = sem("seat_chain")
        rows_sent = sem("rows_sent")
        post_const = sem("post_const")
        table = sem("table")
        counted = sem("counted")
        pad_sent = sem("pad_sent")
        gating = sem("gating")
        gate_exp = sem("gate_exp")
        tile_loaded = sem("tile_loaded")
        turned = sem("turned")
        xs_high_done = sem("xs_high_done")
        xs_low_done = sem("xs_low_done")
        up_done = sem("up_done")
        hid_high = sem("hid_high")
        hid_low = sem("hid_low")
        down_done = sem("down_done")
        meta_chain = sem("meta_chain")
        dest_ready = sem("dest_ready")
        y_copied = sem("y_copied")
        y_sent = sem("y_sent")
        fin_loaded = [sem(f"fin_loaded{i}") for i in range(2)]
        fx_loaded = sem("fx_loaded")
        fin_chain = sem("fin_chain")
        fin_scale = sem("fin_scale")
        fin_ready = sem("fin_ready")
        fin_stored = [sem(f"fin_stored{i}") for i in range(2)]

        AHEAD = 2
        FOLDS = 4
        CHOICE_STEPS, SEAT_STEPS, TABLE_STEPS = 6, 5, 14
        GELU_STEPS, SIGMOID_STEPS, STAT_STEPS, SCALE_STEPS = 3, 3, 2, 3
        FIN_STEPS = 2 + STAT_STEPS

        block = es.enter_context(nc.Block())

        def wait(eng, s, value):
            if not isinstance(value, int) or value > 0:
                eng.wait_ge(s, value)

        def pipeline(eng, body):
            for i in range(-1, 4):
                body(i, Stages(i, NB))
            with eng.Fori(0, NB - 5, 1) as n:
                body(n + 4, Stages(4, NB))
            for i in range(NB - 1, NB + 3):
                body(i, Stages(i, NB))

        def wait_apart(eng, *waits):
            values = [(s, v if isinstance(v, int) else eng.to_reg(v)) for s, v in waits]
            eng.wait_ge(const_ready, 1)
            for s, value in values:
                wait(eng, s, value)

        def at(v, n):
            return v[n] if isinstance(n, int) else v[ds(n, 1)][0]

        def row_of(t, n):
            return t[:, n, :] if isinstance(n, int) else t[:, ds(n, 1), :].rearrange("p a n -> p (a n)")

        def min_of(n):
            return min(n, NB) if isinstance(n, int) else n

        def scored(i, g, st):
            return (i, g + AHEAD, st.cur) if g < G - AHEAD else (i + 1, g + AHEAD - G, st.next)

        @block.sync
        def _(sp):
            def load_stage(e):
                for w, (w_e, chunks) in enumerate(((w1_e, KC), (w2_e, FC))):
                    sp.dma_start(stage[e % STAGES][:, w, :].rearrange("p (k f) -> p k f", k=chunks), w_e[e]).then_inc(stage_loaded[e % STAGES], 16)
            load_stage(0)
            for w_sb, w in ((wq, WqT), (wk, WkT), (wv, WvT)):
                sp.dma_start(w_sb[:, :, :], w.rearrange("(k p) n -> p k n", p=P)).then_inc(lora_loaded, 16)
            sp.dma_start(bqk[:, 0, :], bq).then_inc(lora_loaded, 16)
            sp.dma_start(bqk[:, 1, :], bk).then_inc(lora_loaded, 16)
            sp.dma_start(bv_all[:, :], bv.rearrange("(a n) -> a n", a=1).to_broadcast([P, C])).then_inc(lora_loaded, 16)
            sp.dma_start(wg[:, :, :], Wg.rearrange("(k p) e -> p k e", p=P)).then_inc(lora_loaded, 16)
            for n, a in enumerate((Aq, Ak, Av)):
                sp.dma_start(lora_a[:, n, :], a).then_inc(lora_loaded, 16)
            for n, b in enumerate((BqT, BkT, BvT, BoT)):
                sp.dma_start(lora_b[:, n, :], b).then_inc(lora_loaded, 16)
            sp.wait_ge(const_ready, 1)
            wo_v = WoT.rearrange("(g j d) n -> j d g n", g=G, j=HG)
            for j in range(HG):
                sp.dma_start(wo[j * HR:j * HR + D, :, :], wo_v[j]).then_inc(wo_loaded, 16)
            sp.dma_start(wo[D:D + 1, 0, :], bo.rearrange("(a n) -> a n", a=1)).then_inc(wo_loaded, 16)
            sp.dma_start(lora_ao[:, :, :].rearrange("r g (j z) -> r (g j) z", z=HR)[:, :, 0:D],
                         Ao.rearrange("r (h d) -> r h d", d=D)).then_inc(wo_loaded, 16)
            for e in range(1, STAGES):
                load_stage(e)
            for e in range(STAGES, E):
                sp.wait_ge(low_done, 2 * (e - STAGES + 1))
                load_stage(e)
            sp.wait_ge(low_done, 2 * E)
            sp.wait_ge(scale_done, E + 1)
            sp.wait_ge(fold_done, FOLDS)

            def set_maxima(sb_, sg):
                sp.wait_ge(mT_copied, G * sb_ + sg + 1)
                sp.dma_start(qs[MROW:KROWS, sg, :, :].bitcast(F32), mT[:, :]).then_inc(mrow_set[sg], 16)

            def body(i, st):
                b = i + 1
                if st.next:
                    wait(sp, v_proj, b)
                    sp.dma_start(xT_sb[:, :, :], at(x_ch, b)).then_inc(xT_loaded, 16)
                if st.post:
                    wait(sp, x1_ready, i - 1)
                    sp.dma_start(x_sb[:, :, :], at(x_tok, i - 1)).then_inc(x_loaded, 16)
                    wait(sp, h_done, i - 1)
                    sp.dma_start(cT[:, :, :], at(ctx_ch, i - 1)).then_inc(cT_loaded, 16)
                if st.cross:
                    wait(sp, xo_done, i - 2)
                    sp.dma_start(cr[:, :], at(ctx, i - 2)).then_inc(cr_loaded, 16)
                for g in range(G):
                    sb_, sg, s_on = scored(i, g, st)
                    if s_on and g < KC:
                        set_maxima(sb_, sg)
                    if st.next and g < KC:
                        wait_apart(sp, (qk_low, KC * b + g + 1), *((slot_loaded[gg], 64 * b) for gg in (2 * g, 2 * g + 1)))
                        heads = slice(g * P // D, (g + 1) * P // D)
                        for scratch, s, src in ((q_parts, 0, 0), (q_parts, 1, 1), (q_parts, 2, 0),
                                                (k_parts, 0, 2), (k_parts, 1, 3)):
                            sp.dma_start(scratch[heads, s], part[:, src, :].bitcast(F32)).then_inc(part_sent[g], 16)
                    if g == 2 and st.cross:
                        sp.wait_ge(x2_ready, i - 1)
                        x2_v = x2_rows.rearrange("(b c p) n -> b p c n", p=P, c=TC)
                        sp.dma_start(at(x2_v, i - 2), x2[:, :, 0:C]).then_inc(x2_stored, 16)
                    if st.next:
                        wait_apart(sp, (part_sent[g // 2], 80 * (b + 1)), (st_done, H * i + HG * (g + 1)))
                        hd = slice(g * HG, (g + 1) * HG)
                        for dst, row, src in ((qs, 0, q_rows[0:2 * D, hd]), (qs, 2 * D, q_rows[D:3 * D, hd]),
                                              (ks, 0, k_rows[:, hd]), (ks, 2 * D, k_rows[:, hd])):
                            sp.dma_start(dst[row:row + 2 * D, g, :, :].bitcast(F32), src).then_inc(slot_loaded[g], 16)
                    if s_on and g >= KC:
                        set_maxima(sb_, sg)
            pipeline(sp, body)

            def load_tile(t):
                row = sp.value_load(tab[0:1, 1, t:t + 1] if isinstance(t, int) else tab[0:1, 1, ds(t, 1)],
                                    min_val=0, max_val=E * CAP - ET)
                sp.dma_start(xt[:, :, :], sent[ds(row, ET), :].rearrange("(c p) n -> p c n", p=P)).then_inc(tile_loaded, 16)
            sp.wait_ge(counted, 1)
            sp.wait_ge(post_const, 2)
            sp.wait_ge(rows_sent, 64 * NB)
            for e in range(E):
                row = sp.value_load(cnt_i[0:1, e:e + 1], min_val=0, max_val=E * CAP - ET)
                sp.dma_start(sent[ds(row, ET), :].rearrange("(c p) n -> p c n", p=P), pad[:, :, :]).then_inc(pad_sent, 16)
            sp.wait_ge(table, TABLE_STEPS)
            sp.wait_ge(pad_sent, 16 * E)
            load_tile(0)
            sp.wait_ge(x2_stored, 16 * NB)
            fx_v = x2_rows.rearrange("(b c p) n -> b p c n", p=P, c=TC)
            with sp.Fori(0, NB, 1) as t:
                sp.wait_ge(turned, t + 1)
                sp.wait_ge(meta_chain, 2 * t + 1)
                load_tile(t + 1)
                sp.dma_start(fx[:, ds(t * TC, TC), :], at(fx_v, t)).then_inc(fx_loaded, 16)
            with sp.Fori(0, TILES - 1 - NB, 1) as n:
                sp.wait_ge(turned, n + NB + 1)
                sp.wait_ge(meta_chain, 2 * (n + NB) + 1)
                load_tile(n + NB + 1)

            sp.wait_ge(y_sent, 16 * ETC * TILES)
            fin_y = [mixed[k * N:(k + 1) * N, :].rearrange("(b c p) n -> b p c n", p=P, c=TC) for k in range(2)]

            def load_fin(n, q):
                b = n * 2 + q
                for k in range(2):
                    sp.dma_start(fy[q][:, k, :, :], at(fin_y[k], b)).then_inc(fin_loaded[q], 16)

            load_fin(0, 0)
            load_fin(0, 1)
            with sp.Fori(0, NB // 2 - 1, 1) as n:
                for q in range(2):
                    sp.wait_ge(fin_chain, FIN_STEPS * (n * 2 + q) + 2)
                    load_fin(n + 1, q)
            for q in range(2):
                sp.wait_ge(fin_stored[q], 16 * NB // 2)

        @block.gpsimd
        def _(pool):
            g = nc.gpsimd
            g.memset(ident[:, :], 0.0)
            g.memset(before[:, :], 1.0)
            g.memset(ones_sq[:, :], 1.0)
            g.memset(eps_col[:, :], EPS)
            g.memset(one_col[:, :], 1.0)
            g.iota(iota_e[:, :], pattern=[[1, E]], base=0, channel_multiplier=0, allow_small_or_imprecise_dtypes=True)
            g.iota(count[:, :], pattern=[[CAP, E]], base=0, channel_multiplier=0, allow_small_or_imprecise_dtypes=True)
            g.iota(token[:, :], pattern=[[P, TC]], base=0, channel_multiplier=1, allow_small_or_imprecise_dtypes=True)
            g.memset(wo[:, :, :], 0.0).then_inc(pool_consts, 1)
            pool.wait_ge(pool_consts, 1)
            g.memset(ones_2[:, :], 1.0).then_inc(pool_consts, 1)
            pool.wait_ge(pool_consts, 2)
            g.memset(lora_ao[:, :, :], 0.0).then_inc(const_ready, 1)
            pool.wait_ge(const_ready, 1)
            g.affine_select(out=ident[:, :], in_=ident[:, :], compare_op=ALU.not_equal, fill=1.0,
                            base=0, pattern=[[-1, P]], channel_multiplier=1)
            g.affine_select(out=before[:, :], in_=before[:, :], compare_op=ALU.is_gt, fill=0.0,
                            base=0, pattern=[[1, P]], channel_multiplier=-1).then_inc(const_ready, 1)
            pool.wait_ge(low_done, 2 * E)
            pool.wait_ge(scale_done, E + 1)
            pool.wait_ge(fold_done, FOLDS)
            g.memset(ks[MROW:KROWS, :, :, :].bitcast(F32), 1.0).then_inc(rows_const, 1)
            pool.wait_ge(rows_const, 1)
            g.memset(va[:, :, :, D:HR], 1.0).then_inc(rows_const, 1)
            pool.wait_ge(rows_const, 2)

            def body(i, st):
                if st.cross:
                    wait_apart(pool, (h_copied, i - 1), (mrow_zero, G * min_of(i + 1)))
                    link = Chain(pool, gelu_in, i - 2, GELU_STEPS)
                    link(g.tensor_scalar(hu, hu, 1.0, None, ALU.add), wait_apart)
                    link(g.tensor_tensor(hu, hu, hv, ALU.mult), wait_apart)
                    link(g.tensor_scalar(hu, hu, GELU_LEAST, None, ALU.max), wait_apart)
                    wait_apart(pool, (sigmoid, SIGMOID_STEPS * (i - 1)))
                    g.tensor_tensor(hv, hu, hv, ALU.mult).then_inc(gelu_out, 1)
                    wait_apart(pool, (gelu_out, i - 1))
                for gr in range(G):
                    if st.next:
                        wait_apart(pool, (st_done, H * i + HG * (gr + 1)))
                        g.memset(qs[MROW:KROWS, gr, :, :].bitcast(F32), 0.0).then_inc(mrow_zero, 1)
                    if gr == 0 and st.send:
                        wait_apart(pool, (seat_chain, SEAT_STEPS * (i - 2)))
                        for k in range(2):
                            for c in range(TC):
                                g.indirect_dma_start(
                                    out=sent, out_offset=bass.IndirectOffsetOnAxis(seat_i[:, k, c:c + 1], 0),
                                    in_=x2[:, c, :], in_offset=None).then_inc(rows_sent, 16)
            pipeline(pool, body)

            pool.wait_ge(rows_sent, 64 * NB)
            g.memset(pad[:, :, :], 0.0).then_inc(post_const, 1)
            pool.wait_ge(post_const, 1)
            g.memset(pad[:, :, C:C + 1], float(DROP))
            g.memset(ones_e[:, :], 1.0)
            g.iota(fulls[:, :], pattern=[[ET, N // ET]], base=0, channel_multiplier=0, allow_small_or_imprecise_dtypes=True)
            g.iota(tau[:, :], pattern=[[1, TILES]], base=0, channel_multiplier=0,
                   allow_small_or_imprecise_dtypes=True).then_inc(post_const, 1)
            with pool.Fori(0, TILES, 1) as t:
                wait_apart(pool, (y_copied, t + 1), (dest_ready, t + 1))
                for c in range(ETC):
                    g.indirect_dma_start(
                        out=mixed, out_offset=bass.IndirectOffsetOnAxis(dest[:, c:c + 1], 0),
                        in_=ys[:, c, :], in_offset=None, bounds_check=2 * N - 1, oob_is_err=False).then_inc(y_sent, 16)

        @block.scalar
        def _(act):
            a = nc.scalar
            a.preload_act_table_set("natural_log_exp_and_others")
            for e in range(E):
                act.wait_ge(scale_done, e + 1)
                for w in range(2):
                    a.activation(w_high[w][:, e, :], stage[e % STAGES][:, w, :], ACT.Identity,
                                 scale=winv[:, 2 * e + w:2 * e + w + 1]).then_inc(high_done, 1)

            def norm_scale(link, stats, log_var, minus, to):
                a.activation(minus, stats[:, :, 0:1], ACT.Copy, scale=-1.0)
                link(a.activation(log_var, stats[:, :, 1:2], ACT.Ln, bias=eps_col[:, 0:1]))
                link(a.activation(to[:, :, 0:1], log_var, ACT.Exp, scale=-0.5))
                for c in range(TC):
                    last = a.activation(to[:, c, 1:2], minus[:, c, :], ACT.Copy, scale=to[:, c, 0:1])
                link(last)
                link.end()

            def inverse_sums(piece, pair):
                act.wait_ge(den_ready, piece + 1)
                flat = on[:, pair:pair + 2, :].rearrange("p g t -> p (g t)")
                link = Chain(act, den_log, piece, 1)
                link(a.activation(flat, flat, ACT.Ln))
                a.activation(flat, flat, ACT.Exp, scale=-1.0).then_inc(den_inverse, 1)

            def body(i, st):
                b = i + 1
                for g in range(G):
                    sb_, sg, s_on = scored(i, g, st)
                    for j in range(HG):
                        if st.cur:
                            act.wait_ge(st_done, H * i + HG * g + j + 1)
                            wait(act, pv_done, G * i + g)
                            a.activation(pt[:, j, :], ST[j % 2][:, :], ACT.Exp).then_inc(exp_done, 1)
                        if g == 3 and st.post and j < TC:
                            last = a.activation(x1[:, j, :], x_sb[:, j, :], ACT.Identity, bias=rstd[:, 0, j, 1:2],
                                                scale=rstd[:, 0, j, 0:1])
                            if j == TC - 1:
                                last.then_inc(x1_ready, 1)
                    if g == 0 and st.cross:
                        act.wait_ge(gelu_in, GELU_STEPS * (i - 1))
                        link = Chain(act, sigmoid, i - 2, SIGMOID_STEPS)
                        link(a.activation(hu, hu, ACT.Exp, scale=-2.0 * GELU_C))
                        link(a.activation(hu, hu, ACT.Ln, bias=one_col[0:S2, 0:1]))
                        link(a.activation(hu, hu, ACT.Exp, scale=-1.0))
                    if g == 0 and st.post:
                        inverse_sums(2 * i - 1, 2)
                    if g == 3 and st.cur:
                        inverse_sums(2 * i, 0)
                    if g == 3 and st.post:
                        act.wait_ge(x1T_done, i)
                        a.activation(x1T[:, :, :].rearrange("p k t -> p (k t)"), M[1][:, :], ACT.Copy).then_inc(x1T_copied, 1)
                    if g == 2 and st.cross:
                        act.wait_ge(x2T_done, i - 1)
                        a.activation(x2T[:, :, :].rearrange("p k t -> p (k t)"), M[0][:, :], ACT.Copy).then_inc(x2T_copied, 1)
                    if s_on:
                        act.wait_ge(mT_done, G * sb_ + sg + 1)
                        wait(act, mrow_set[sg - 1], 16 * (sb_ + 1) if sg else 16 * sb_)
                        a.activation(mT[:, :], M[1][0:2 * HG, 0:T], ACT.Copy).then_inc(mT_copied, 1)
                    if g < KC and st.next:
                        act.wait_ge(qk_proj, KC * b + g + 1)
                        wait(act, part_sent[1 - g], 80 * (b + g))
                        for n in range(2):
                            last = a.activation(part[:, 2 * n, :], M[0][:, n * T:(n + 1) * T], ACT.Identity,
                                                bias=bqk[:, n, g:g + 1])
                        last.then_inc(qk_high, 1)
                    if g == 1 and st.cross:
                        act.wait_ge(ln2_stats, STAT_STEPS * (i - 1))
                        norm_scale(Chain(act, ln2_scale, i - 2, SCALE_STEPS), mv[:, 1], lnv[:, 1], neg[:, 1], rstd[:, 1])
                        wait(act, x2_stored, 16 * (i - 2))
                        wait(act, rows_sent, 64 * (i - 2))
                        for c in range(TC):
                            last = a.activation(x2[:, c, 0:C], x1[:, c, :], ACT.Identity, bias=rstd[:, 1, c, 1:2],
                                                scale=rstd[:, 1, c, 0:1])
                        last.then_inc(x2_ready, 1)
                    if g == 2 and st.post:
                        act.wait_ge(ln1_stats, STAT_STEPS * i)
                        norm_scale(Chain(act, ln1_scale, i - 1, SCALE_STEPS), mv[:, 0], lnv[:, 0], neg[:, 0], rstd[:, 0])
                    if g == 2 and st.cross:
                        act.wait_ge(lg_done, i - 1)
                        wait(act, choice, CHOICE_STEPS * (i - 2))
                        a.activation(lg[:, :, :].rearrange("p c e -> p (c e)"), M[1][:, T:T + TC * E], ACT.Copy).then_inc(lg_copied, 1)
                    if g == 3 and (st.post or st.cross):
                        act.wait_ge(h_done, i)
                    if g == 3 and st.post:
                        a.activation(hv, M[1][0:S2, 0:T], ACT.Copy)
                        a.activation(hu, M[1][0:S2, 0:T], ACT.Square, scale=GELU_A ** 0.5).then_inc(h_copied, 1)
                    if g == 3 and st.cross:
                        wait(act, seat_chain, SEAT_STEPS * (i - 2))
                        a.activation(cum[:, :, :].rearrange("p c e -> p (c e)"), M[1][:, CUM:CUM + 3 * E], ACT.Copy).then_inc(cum_copied, 1)
            pipeline(act, body)

            act.wait_ge(gating, 3)
            a.activation(gate[:, :, :], gate[:, :, :], ACT.Exp).then_inc(gate_exp, 1)

            def turn(t):
                act.wait_ge(turned, t + 1)
                a.activation(xs[0][:, :, :].rearrange("p k t -> p (k t)"), XB[:, :], ACT.Copy, scale=XS).then_inc(xs_high_done, 1)

            def tile(t, more):
                for q in range(FC // 2):
                    act.wait_ge(up_done, FC // 2 * t + q + 1)
                    a.activation(hs[0][:, 2 * q:2 * q + 2, :].rearrange("p f t -> p (f t)"), HB[q][:, :], ACT.Relu).then_inc(hid_high, 1)
                if more:
                    turn(t + 1)
                act.wait_ge(down_done, t + 1)
                wait(act, y_sent, 16 * ETC * t)
                for c in range(ETC):
                    last = a.activation(ys[:, c, :], YB[c][:, 0:C], ACT.Copy)
                last.then_inc(y_copied, 1)
            turn(0)
            tile(0, True)
            with act.Fori(0, TILES - 2, 1) as t:
                tile(t + 1, True)
            tile(TILES - 1, False)

            out_v = out.rearrange("b (c p) n -> b p c n", p=P)

            def fin(n, q):
                act.wait_ge(fin_chain, FIN_STEPS * (2 * n + q + 1))
                norm_scale(Chain(act, fin_scale, 2 * n + q, SCALE_STEPS), fmv[:, q], flnv[:, q], fneg[:, q], frs[:, q])
                wait(act, fin_stored[q], 16 * n)
                for c in range(TC):
                    a.activation(fo[q][:, c, :], row_of(fx, 2 * (2 * n + q) + c), ACT.Identity, bias=frs[:, q, c, 1:2],
                                 scale=frs[:, q, c, 0:1]).then_inc(fin_ready, 1)
                act.wait_ge(fin_ready, TC * (2 * n + q + 1))
                act.dma_start(at(out_v, 2 * n + q), fo[q][:, :, :]).then_inc(fin_stored[q], 16)
            for q in range(2):
                fin(0, q)
            with act.Fori(0, NB // 2 - 1, 1) as n:
                for q in range(2):
                    fin(n + 1, q)

        @block.vector
        def _(dve):
            v = nc.vector
            def greatest(e):
                dve.wait_ge(stage_loaded[e % STAGES], 32 * (e // STAGES + 1))
                v.tensor_reduce(absmax[:, :], stage[e % STAGES][:, :, :], AX.X, ALU.max, apply_absolute_value=True).then_inc(absmax_done, 1)

            def low_parts(e):
                for w in range(2):
                    dve.wait_ge(high_done, 2 * e + w + 1)
                    v.scalar_tensor_tensor(w_low[w][:, e, :], stage[e % STAGES][:, w, :], winv[:, 2 * e + w:2 * e + w + 1],
                                           w_high[w][:, e, :], ALU.mult, ALU.subtract).then_inc(low_done, 1)
            greatest(0)
            dve.wait_ge(lora_loaded, 16 * 14)
            dve.wait_ge(wo_loaded, 16 * 6)
            for n, w_sb in enumerate((wq, wk, wv)):
                dve.wait_ge(lora_done, n + 1)
                flat = w_sb[:, :, :].rearrange("p k n -> p (k n)")
                last = v.scalar_tensor_tensor(flat, (S[0], S[1], ST[0])[n][:, :], LORA, flat, ALU.mult, ALU.add)
                if n:
                    last.then_inc(fold_done, 1)
                else:
                    link = Chain(dve, fold_chain, 0, 1)
                    link(last)
                    v.tensor_scalar(flat, flat, float(D) ** -0.5, None, ALU.mult)
                    v.tensor_scalar(bqk[:, 0, :], bqk[:, 0, :], float(D) ** -0.5, None, ALU.mult).then_inc(fold_done, 1)
            dve.wait_ge(lora_done, 4)
            for n, bank in enumerate((ST[1], PV[0])):
                flat = wo[:, 2 * n:2 * n + 2, :].rearrange("p k n -> p (k n)")
                last = v.scalar_tensor_tensor(flat, bank[:, :], LORA, flat, ALU.mult, ALU.add)
            last.then_inc(fold_done, 1)
            for e in range(E):
                link = Chain(dve, diag_chain, e, 1)
                dve.wait_ge(absmax_turned, e + 1)
                link(v.tensor_reduce(peak[:, :], M[0][0:2, 0:P], AX.X, ALU.max))
                v.tensor_scalar(diag[:, :], ident[0:2, 0:2], peak[:, 0:1], None, ALU.mult).then_inc(diag_done, 1)
                dve.wait_ge(peak_spread, e + 1)
                link = Chain(dve, scale_chain, e, 2)
                pw = wpow[:, 2 * e:2 * e + 2]
                link(v.tensor_scalar(pw, M[1][:, 0:2], 2.0 ** -60, None, ALU.max))
                link(v.tensor_scalar(pw.bitcast(I32), pw.bitcast(I32), EXP_MASK, None, ALU.bitwise_and))
                v.tensor_scalar(winv[:, 2 * e:2 * e + 2].bitcast(I32), pw.bitcast(I32), -1.0, float((254 + 4) * EXP_ONE),
                                ALU.mult, ALU.add).then_inc(scale_done, 1)
                if e:
                    low_parts(e - 1)
                if e + 1 < E:
                    greatest(e + 1)
            low_parts(E - 1)
            pw_v = wpow[:, :].rearrange("p (e w) -> p e w", w=2)
            v.scalar_tensor_tensor(yscale[:, :], pw_v[:, :, 0], 1.0 / (XS * WS * WS), pw_v[:, :, 1],
                                   ALU.mult, ALU.mult).then_inc(scale_done, 1)

            def norm_stats(eng_sem, piece, z, which, z_done, z_count, part):
                if part == 0:
                    wait_apart(dve, (z_done, z_count))
                    for c in range(TC):
                        last = v.bn_stats(bn[:, which, c, :], z[:, c, :])
                else:
                    wait_apart(dve, (eng_sem, piece * STAT_STEPS + 1))
                    for c in range(TC):
                        last = v.bn_aggr(mv[:, which, c, :], bn[:, which, c, :])
                last.then_inc(eng_sem, 1)

            def later(eng, what):
                pass

            def flat_of(t):
                return t[:, :, :].rearrange("p c n -> p (c n)")

            def sums_beside(i, pair):
                wait_apart(dve, (pv_done, G * i + 2 - pair), (o_done, i - pair // 2))
                flat = on[:, pair:pair + 2, :].rearrange("p g t -> p (g t)")
                v.stream_shuffle(flat, PV[pair // 2][:, :], [r + D if r < D else r for r in range(HR)]).then_inc(den_ready, 1)

            def divide(piece, pair):
                dve.wait_ge(den_inverse, piece + 1)
                flat = on[:, pair:pair + 2, :].rearrange("p g t -> p (g t)")
                v.tensor_tensor(flat, PV[pair // 2][:, :], flat, ALU.mult).then_inc(norm_done, 1)

            def choose(i):
                dve.wait_ge(lg_copied, i - 1)
                c0 = ds((i - 2) * TC, TC) if not isinstance(i, int) else slice((i - 2) * TC, (i - 1) * TC)
                wait(dve, rows_sent, 64 * (i - 2))
                link = Chain(dve, choice, i - 2, CHOICE_STEPS)
                v.tensor_copy(logits[:, c0, :], lg[:, :, :])
                for c in range(TC):
                    last = v.max(lg8[:, c, :], lg[:, c, :])
                link(last, wait_apart)
                for c in range(TC):
                    last = v.max_index(ix8[:, c, :], lg8[:, c, :], lg[:, c, :])
                link(last)
                for k in range(2):
                    last = v.tensor_tensor(pick[:, k, :, :], iota_e[:, :].unsqueeze(1).to_broadcast([P, TC, E]),
                                           ix8[:, :, k:k + 1].to_broadcast([P, TC, E]), ALU.is_equal)
                link(last)
                v.tensor_copy(picked[:, :, c0], ix8[:, :, 0:2].rearrange("p c k -> p k c"))
                v.tensor_copy(x2[:, :, C], token[:, :])
                link(v.tensor_tensor(mask[:, :, :], pick[:, 0], pick[:, 1], ALU.add))
                link(v.tensor_copy(x2[:, :, C + 1], ix8[:, :, 0]))
                link(v.tensor_scalar(token[:, :], token[:, :], float(T), None, ALU.add))

            def seat_rows(i, part):
                link = Chain(dve, seat_chain, i - 3, SEAT_STEPS)
                link.n = (0, 2, 3, 4)[part]
                if part == 0:
                    dve.wait_ge(cum_copied, i - 2)
                    link(v.tensor_tensor(seat[:, :, :], cum[:, 0:TC, :], count[:, :].unsqueeze(1).to_broadcast([P, TC, E]), ALU.add))
                    link(v.tensor_tensor(count[:, :], cum[:, TC, :], count[:, :], ALU.add), later)
                elif part == 1:
                    for k in range(2):
                        last = v.tensor_tensor(pick[:, k], pick[:, k], seat[:, :, :], ALU.mult)
                    link(last, later)
                elif part == 2:
                    dve.wait_ge(seat_chain, link.base + 3)
                    link(v.tensor_reduce(seat_k[:, :, :], pick[:, :, :, :], AX.X, ALU.add), later)
                else:
                    dve.wait_ge(seat_chain, link.base + 4)
                    wait(dve, rows_sent, 64 * (i - 3))
                    link(v.tensor_copy(seat_i[:, :, :], seat_k[:, :, :]), later)

            def first_half(i, g, st):
                if g == 1 and st.cross:
                    dve.wait_ge(xo_done, i - 1)
                    v.tensor_tensor(flat_of(x1), M[1][:, :], flat_of(x1), ALU.add).then_inc(z2_done, 1)
                if g == 2 and st.post:
                    dve.wait_ge(o_done, i)
                    dve.wait_ge(x_loaded, 16 * i)
                    v.tensor_tensor(flat_of(x_sb), M[1][:, :], flat_of(x_sb), ALU.add).then_inc(z1_done, 1)

            def body(i, st):
                b = i + 1
                for g in range(G):
                    sb_, sg, s_on = scored(i, g, st)
                    for j in range(HG):
                        if g == 0 and st.send:
                            seat_rows(i, j)
                        if j == 1:
                            first_half(i, g, st)
                        if g == 1 and st.cross and j >= 2:
                            norm_stats(ln2_stats, i - 2, x1, 1, z2_done, i - 1, j - 2)
                        if g == 2 and st.post and j >= 2:
                            norm_stats(ln1_stats, i - 1, x_sb, 0, z1_done, i, j - 2)
                        if s_on:
                            dve.wait_ge(s_done, H * sb_ + HG * sg + j + 1)
                            v.tensor_reduce(mx[:, :, j], S[j % 2][:, :].rearrange("p (c t) -> p c t", c=TC), AX.X,
                                            ALU.max, negate=True).then_inc(max_done, 1)
                    if s_on:
                        dve.wait_ge(max_done, H * sb_ + HG * (sg + 1))
                        wait(dve, mT_done, G * sb_ + sg)
                        link = Chain(dve, msplit, G * sb_ + sg, 2)
                        link(v.tensor_copy(mm[:, :, 0:HG], mx[:, :, :]))
                        v.tensor_tensor(mm[:, :, HG:2 * HG], mx[:, :, :], mm[:, :, 0:HG].bitcast(F32), ALU.subtract).then_inc(msplit, 1)
                    if g == 3 and st.cross:
                        choose(i)
                    if g == 3 and st.cur:
                        divide(2 * i, 0)
                    if g == 2 and st.cur:
                        sums_beside(i, 0)
                    if g == 0 and st.post:
                        sums_beside(i, 2)
                        divide(2 * i - 1, 2)
                    if g < KC and st.next:
                        dve.wait_ge(qk_high, KC * b + g + 1)
                        for n in range(2):
                            last = v.scalar_tensor_tensor(part[:, 2 * n + 1, :], M[0][:, n * T:(n + 1) * T], bqk[:, n, g:g + 1],
                                                          part[:, 2 * n, :].bitcast(F32), ALU.add, ALU.subtract)
                        last.then_inc(qk_low, 1)
                    if g == 3 and st.next:
                        dve.wait_ge(v_proj, b + 1)
                        wait(dve, pv_done, G * b)
                        for c in range(TC):
                            last = v.tensor_tensor(va[:, c, :, 0:D], M[0][:, c * C:(c + 1) * C].rearrange("p (h d) -> p h d", d=D),
                                                   bv_all[:, :].rearrange("p (h d) -> p h d", d=D), ALU.add)
                        last.then_inc(v_ready, 1)
            pipeline(dve, body)

            v.tensor_copy(cnt_i[:, :], count[:, :]).then_inc(counted, 1)
            dve.wait_ge(post_const, 2)
            link = Chain(dve, table, 0, TABLE_STEPS)
            link(v.scalar_tensor_tensor(num[:, :], iota_e[:, :], -float(CAP), count[:, :], ALU.mult, ALU.add))
            link(v.tensor_tensor(over[:, :, :], num[:, :].unsqueeze(2).to_broadcast([P, E, N // ET]),
                                 fulls[:, :].unsqueeze(1).to_broadcast([P, E, N // ET]), ALU.is_gt))
            link(v.tensor_reduce(tiles_of[:, :], over[:, :, :], AX.X, ALU.add))
            link(v.tensor_tensor_scan(last_of[:, :], ones_e[:, :], tiles_of[:, :], 0.0, ALU.mult, ALU.add))
            link(v.tensor_tensor(base_of[:, :], tiles_of[:, :], last_of[:, :], ALU.subtract))
            link(v.tensor_scalar(base_of[:, :], base_of[:, :], float(ET), None, ALU.mult))
            link(v.scalar_tensor_tensor(base_of[:, :], iota_e[:, :], float(CAP), base_of[:, :], ALU.mult, ALU.add))
            link(v.tensor_scalar(num[:, 0:1], last_of[:, E - 1:E], -1.0, None, ALU.add))
            link(v.tensor_scalar(tau[:, :], tau[:, :], num[:, 0:1], None, ALU.min))
            link(v.tensor_tensor(by_e[:, :, :], last_of[:, :].unsqueeze(1).to_broadcast([P, TILES, E]),
                                 tau[:, :].unsqueeze(2).to_broadcast([P, TILES, E]), ALU.is_le))
            link(v.tensor_reduce(tile_e[:, :], by_e[:, :, :], AX.X, ALU.add))
            v.tensor_copy(tab[:, 0, :], tile_e[:, :])
            link(v.tensor_tensor(by_e[:, :, :], iota_e[:, :].unsqueeze(1).to_broadcast([P, TILES, E]),
                                 tile_e[:, :].unsqueeze(2).to_broadcast([P, TILES, E]), ALU.is_equal))
            v.tensor_tensor(by_e[:, :, :], by_e[:, :, :], base_of[:, :].unsqueeze(1).to_broadcast([P, TILES, E]),
                            ALU.mult).then_inc(gating, 1)
            dve.wait_ge(gating, 1)
            link(v.tensor_reduce(tile_row[:, :], by_e[:, :, :], AX.X, ALU.add))
            link(v.scalar_tensor_tensor(tab[:, 1, :], tau[:, :], float(ET), tile_row[:, :], ALU.mult, ALU.add))
            link.end()

            def spread(t):
                return t.unsqueeze(2).to_broadcast([P, NT, E])

            def gating_weights():
                n = [1]

                def link(ins):
                    n[0] += 1
                    ins.then_inc(gating, 1)
                    dve.wait_ge(gating, n[0])
                for k in range(2):
                    v.tensor_tensor(chosen[:, k], iota_e[:, :].unsqueeze(1).to_broadcast([P, NT, E]), spread(picked[:, k, :]), ALU.is_equal)
                link(v.tensor_reduce(gmax[:, :], logits[:, :, :], AX.X, ALU.max))
                link(v.tensor_tensor(gate[:, :, :], logits[:, :, :], spread(gmax[:, :]), ALU.subtract))
                dve.wait_ge(gate_exp, 1)
                link(v.tensor_reduce(gsum[:, :], gate[:, :, :], AX.X, ALU.add))
                link(v.reciprocal(gsum[:, :], gsum[:, :]))
                link(v.tensor_tensor(gate[:, :, :], gate[:, :, :], spread(gsum[:, :]), ALU.mult))
                for k in range(2):
                    last = v.tensor_tensor(gprod[:, k, :, :], chosen[:, k, :, :], gate[:, :, :], ALU.mult)
                link(last)
                link(v.tensor_reduce(weight[:, :, :], gprod[:, :, :, :], AX.X, ALU.add))
                link(v.scalar_tensor_tensor(gsum[:, :], weight[:, 0, :], 1e-9, weight[:, 1, :], ALU.add, ALU.add))
                link(v.reciprocal(gsum[:, :], gsum[:, :]))
                for k in range(2):
                    last = v.tensor_tensor(gprod[:, k, :, :], chosen[:, k, :, :], yscale[:, :].unsqueeze(1).to_broadcast([P, NT, E]), ALU.mult)
                link(last)
                link(v.tensor_reduce(gscale[:, :, :], gprod[:, :, :, :], AX.X, ALU.add))
                link(v.tensor_tensor(weight[:, :, :], weight[:, :, :], gsum[:, :].unsqueeze(1).to_broadcast([P, 2, NT]), ALU.mult))
                link(v.tensor_tensor(weight[:, :, :], weight[:, :, :], gscale[:, :, :], ALU.mult))
            gating_weights()

            def turn(t):
                dve.wait_ge(xs_high_done, t + 1)
                v.scalar_tensor_tensor(xs[1][:, :, :].rearrange("p k t -> p (k t)"), XB[:, :], XS,
                                       xs[0][:, :, :].rearrange("p k t -> p (k t)"), ALU.mult, ALU.subtract).then_inc(xs_low_done, 1)

            def halves(t):
                dve.wait_ge(tile_loaded, 16 * (t + 1))
                wait(dve, dest_ready, t)
                link = Chain(dve, meta_chain, t, 2)
                link(v.tensor_copy(meta_next[:, :, :], xt[:, :, C:ROW]))
                e_col = tile_e[:, t:t + 1] if isinstance(t, int) else tile_e[:, ds(t, 1)]
                link(v.tensor_scalar(other[:, :], meta_next[:, :, 1], e_col, float(N), ALU.not_equal, ALU.mult))

            def tile(t, more):
                halves(t)
                for q in range(FC // 2):
                    dve.wait_ge(hid_high, FC // 2 * t + q + 1)
                    v.scalar_tensor_tensor(hs[1][:, 2 * q:2 * q + 2, :].rearrange("p f t -> p (f t)"), HB[q][:, :], 0.0,
                                           hs[0][:, 2 * q:2 * q + 2, :].rearrange("p f t -> p (f t)"),
                                           ALU.max, ALU.subtract).then_inc(hid_low, 1)
                wait(dve, y_sent, 16 * ETC * t)
                v.tensor_tensor(dest[:, :], other[:, :], meta_next[:, :, 0], ALU.add).then_inc(dest_ready, 1)
                if more:
                    turn(t + 1)
            turn(0)
            tile(0, True)
            with dve.Fori(0, TILES - 2, 1) as t:
                tile(t + 1, True)
            tile(TILES - 1, False)

            def fin(n, q):
                dve.wait_ge(fin_loaded[q], 32 * (n + 1))
                wait(dve, fin_scale, SCALE_STEPS * (2 * n + q - 1))
                link = Chain(dve, fin_chain, 2 * n + q, FIN_STEPS)
                for k in range(2):
                    for c in range(TC):
                        z = row_of(fx, 2 * (2 * n + q) + c)
                        w_col = weight[:, k, ds(2 * (2 * n + q) + c, 1)]
                        last = v.scalar_tensor_tensor(z, fy[q][:, k, c, :], w_col, z, ALU.mult, ALU.add)
                    link(last, wait_apart)
                for c in range(TC):
                    last = v.bn_stats(fbn[:, q, c, :], row_of(fx, 2 * (2 * n + q) + c))
                link(last, wait_apart)
                for c in range(TC):
                    last = v.bn_aggr(fmv[:, q, c, :], fbn[:, q, c, :])
                link(last)
                link.end()
            dve.wait_ge(fx_loaded, 16 * NB)
            for q in range(2):
                fin(0, q)
            with dve.Fori(0, NB // 2 - 1, 1) as n:
                for q in range(2):
                    fin(n + 1, q)

        @block.tensor
        def _(pe):
            mmul = nc.tensor.matmul
            pe.wait_ge(lora_loaded, 16 * 14)
            pe.wait_ge(wo_loaded, 16 * 6)
            for n in range(3):
                for k in range(KC):
                    last = mmul((S[0], S[1], ST[0])[n][:, k * C:(k + 1) * C], lora_a[:, n, k * P:(k + 1) * P], lora_b[:, n, :],
                                start=True, stop=True)
                last.then_inc(lora_done, 1)
            for g in range(G):
                last = mmul((ST[1], PV[0])[g // 2][:, g % 2 * C:(g % 2 + 1) * C], lora_ao[:, g, :], lora_b[:, 3, :],
                            start=True, stop=True)
            last.then_inc(lora_done, 1)
            pe.wait_ge(const_ready, 2)
            for e in range(E):
                pe.wait_ge(absmax_done, e + 1)
                nc.tensor.transpose(M[0][0:2, 0:P], absmax[:, :], ident[:, :]).then_inc(absmax_turned, 1)
                pe.wait_ge(diag_done, e + 1)
                mmul(M[1][:, 0:2], ones_2[:, :], diag[:, :], start=True, stop=True).then_inc(peak_spread, 1)

            def mixing_bank_free(i, g):
                if g == 0:
                    wait(pe, h_copied, min_of(i - 1))
                    wait(pe, cum_copied, min_of(i - 2))
                elif g == 1:
                    wait(pe, z2_done, min_of(i - 1))
                elif g == 2:
                    wait(pe, z1_done, min_of(i))
                else:
                    wait(pe, lg_copied, min_of(i - 1))

            def turn_rows(bank, rows):
                for k in range(KC):
                    for c in range(TC):
                        last = nc.tensor.transpose(bank[:, k * T + c * P:k * T + (c + 1) * P], rows[:, c, k * P:(k + 1) * P], ident[:, :])
                return last

            def turn_maxima(i, g, sb_, sg):
                pe.wait_ge(msplit, 2 * (G * sb_ + sg + 1))
                mixing_bank_free(i, g)
                wait(pe, mT_copied, G * sb_ + sg)
                for c in range(TC):
                    last = nc.tensor.transpose(M[1][0:2 * HG, c * P:(c + 1) * P], mm[:, c, :].bitcast(F32), ident[:, :])
                last.then_inc(mT_done, 1)

            def count_rows(i):
                pe.wait_ge(choice, CHOICE_STEPS * (i - 1))
                sums = M[1][:, CUM:CUM + 3 * E].rearrange("p (c e) -> p c e", e=E)
                mmul(sums[:, 0, :], before[:, :], mask[:, 0, :], start=True, stop=True)
                mmul(sums[:, 1, :], before[:, :], mask[:, 1, :], start=True, stop=False)
                mmul(sums[:, 1, :], ones_sq[:, :], mask[:, 0, :], start=False, stop=True)
                mmul(sums[:, 2, :], ones_sq[:, :], mask[:, 0, :], start=True, stop=False)
                return mmul(sums[:, 2, :], ones_sq[:, :], mask[:, 1, :], start=False, stop=True)

            def mix(i, g):
                pe.wait_ge(exp_done, H * i + HG * (g + 1))
                pe.wait_ge(v_ready, i + 1)
                if g % 2 == 0:
                    wait(pe, norm_done, 2 * i + g // 2 - 1)
                for c in range(TC):
                    for j in range(HG):
                        last = mmul(PV[g // 2][j * HR:(j + 1) * HR, g % 2 * T:(g % 2 + 1) * T], va[:, c, g * HG + j, :],
                                    pt[:, j, c * T:(c + 1) * T], start=c == 0, stop=c == TC - 1)
                last.then_inc(pv_done, 1)

            def body(i, st):
                b = i + 1

                def project(g, n):
                    w = (wq, wk)[n]
                    for k in range(KC):
                        last = mmul(M[0][:, n * T:(n + 1) * T], w[:, k, g * P:(g + 1) * P], xT_sb[:, k, :],
                                    start=k == 0, stop=k == KC - 1)
                    return last

                def values(c):
                    for k in range(KC):
                        last = mmul(M[0][:, c * C:(c + 1) * C], xT_sb[:, k, c * P:(c + 1) * P], wv[:, k, :],
                                    start=k == 0, stop=k == KC - 1)
                    return last

                for g in range(G):
                    sb_, sg, s_on = scored(i, g, st)
                    if st.cur:
                        pe.wait_ge(mrow_set[g], 16 * (i + 1))
                    for j in range(HG):
                        if st.cur:
                            wait(pe, exp_done, H * i + HG * g + j - 1)
                            for c in range(TC):
                                last = mmul(ST[j % 2][:, c * T:(c + 1) * T], ks[0:KROWS, g, j, c * P:(c + 1) * P],
                                            qs[0:KROWS, g, j, :], start=True, stop=True)
                            last.then_inc(st_done, 1)
                        if s_on and st.cur:
                            score(sb_, sg, j)
                    if g < KC and st.next:
                        pe.wait_ge(xT_loaded, 16 * (b + 1))
                        wait(pe, v_ready if g == 0 else qk_low, b if g == 0 else 2 * b + 1)
                        project(g, 0)
                    if g == 2 and st.cross:
                        pe.wait_ge(x2_ready, i - 1)
                        if st.next:
                            pe.wait_ge(qk_low, KC * (b + 1))
                        turn_rows(M[0], x2).then_inc(x2T_done, 1)
                    if g < KC and st.next:
                        project(g, 1).then_inc(qk_proj, 1)
                    if s_on and not st.cur:
                        for j in range(HG):
                            score(sb_, sg, j)
                    if g == 3 and st.next:
                        values(1).then_inc(v_proj, 1)
                    if g == 3 and st.post:
                        pe.wait_ge(x1_ready, i)
                        mixing_bank_free(i, g)
                        turn_rows(M[1], x1).then_inc(x1T_done, 1)
                    if st.cur and g >= 1:
                        mix(i, g)
                    if g == 3 and st.post:
                        pe.wait_ge(x1T_copied, i)
                    if s_on:
                        turn_maxima(i, g, sb_, sg)
                    if st.cur and g == 0:
                        mix(i, g)
                    if g == 2 and st.next:
                        if st.cross:
                            pe.wait_ge(x2T_copied, i - 1)
                        else:
                            pe.wait_ge(qk_low, KC * (b + 1))
                        values(0)
                    if s_on:
                        pe.wait_ge(mT_copied, G * sb_ + sg + 1)
                    else:
                        mixing_bank_free(i, g)
                    if g == 0 and st.cross:
                        pe.wait_ge(gelu_out, i - 1)
                        pe.wait_ge(cr_loaded, 16 * (i - 1))
                        for c in range(TC):
                            last = mmul(M[1][:, c * C:(c + 1) * C], hv[:, c * P:(c + 1) * P], cr[:, :], start=True, stop=True)
                        last.then_inc(xo_done, 1)
                    if g == 1 and st.post:
                        pe.wait_ge(norm_done, 2 * i)
                        for c in range(TC):
                            for gg in range(G):
                                last = mmul(M[1][:, c * C:(c + 1) * C], on[:, gg, c * P:(c + 1) * P], wo[:, gg, :],
                                            start=gg == 0, stop=gg == G - 1)
                        last.then_inc(o_done, 1)
                    if g == 2 and st.cross:
                        pe.wait_ge(x2T_copied, i - 1)
                        for c in range(TC):
                            for k in range(KC):
                                last = mmul(M[1][:, T + c * E:T + (c + 1) * E], x2T[:, k, c * P:(c + 1) * P], wg[:, k, :],
                                            start=k == 0, stop=k == KC - 1)
                        last.then_inc(lg_done, 1)
                    if g == 3 and st.post:
                        pe.wait_ge(x1T_copied, i)
                        pe.wait_ge(cT_loaded, 16 * i)
                        for k in range(KC):
                            last = mmul(M[1][0:S2, 0:T], cT[:, k, :], x1T[:, k, :], start=k == 0, stop=k == KC - 1)
                    if g == 3 and st.cross:
                        last = count_rows(i)
                    if g == 3 and (st.post or st.cross):
                        last.then_inc(h_done, 1)

            def score(sb_, sg, j):
                if j == 0:
                    pe.wait_ge(slot_loaded[sg], 64 * (sb_ + 1))
                    pe.wait_ge(mrow_zero, G * sb_ + sg + 1)
                wait(pe, max_done, H * sb_ + HG * sg + j - 1)
                for c in range(TC):
                    last = mmul(S[j % 2][:, c * T:(c + 1) * T], qs[0:KROWS, sg, j, c * P:(c + 1) * P],
                                ks[0:KROWS, sg, j, :], start=True, stop=True)
                last.then_inc(s_done, 1)
            pe.wait_ge(rows_const, 2)
            pe.wait_ge(fold_done, FOLDS)
            pe.wait_ge(scale_done, E + 1)
            pipeline(pe, body)

            pe.wait_ge(low_done, 2 * E)
            pe.wait_ge(high_done, 2 * E)

            def turn(t):
                pe.wait_ge(tile_loaded, 16 * (t + 1))
                wait(pe, xs_low_done, t)
                for k in range(KC):
                    for c in range(ETC):
                        last = nc.tensor.transpose(XB[:, k * ET + c * P:k * ET + (c + 1) * P], xt[:, c, k * P:(k + 1) * P], ident[:, :])
                last.then_inc(turned, 1)

            def tile(t, more):
                e = pe.value_load(tab[0:1, 0, t:t + 1] if isinstance(t, int) else tab[0:1, 0, ds(t, 1)], min_val=0, max_val=E - 1)
                pe.wait_ge(xs_low_done, t + 1)
                for q in range(FC // 2):
                    for f in (2 * q, 2 * q + 1):
                        n = 0
                        for k in range(KC):
                            for w, xp in ((w_high[0], xs[0]), (w_high[0], xs[1]), (w_low[0], xs[0])):
                                last = mmul(HB[q][:, f % 2 * ET:(f % 2 + 1) * ET],
                                            w[:, ds(e, 1), k * F + f * P:k * F + (f + 1) * P].rearrange("p a f -> p (a f)"),
                                            xp[:, k, :], start=n == 0, stop=n == 3 * KC - 1)
                                n += 1
                    last.then_inc(up_done, 1)
                if more:
                    turn(t + 1)
                wait(pe, y_copied, t)
                for f in range(FC):
                    if f % 2 == 0:
                        pe.wait_ge(hid_low, FC // 2 * t + f // 2 + 1)
                    for c in range(ETC):
                        for n, (w, hp) in enumerate(((w_high[1], hs[0]), (w_high[1], hs[1]), (w_low[1], hs[0]))):
                            last = mmul(YB[c][:, 0:C], hp[:, f, c * P:(c + 1) * P],
                                        w[:, ds(e, 1), f * C:(f + 1) * C].rearrange("p a f -> p (a f)"),
                                        start=f == 0 and n == 0, stop=f == FC - 1 and n == 2)
                last.then_inc(down_done, 1)
            turn(0)
            tile(0, True)
            with pe.Fori(0, TILES - 2, 1) as t:
                tile(t + 1, True)
            tile(TILES - 1, False)


def kernel(x, ctx_1024, L0_attn_Wq, L0_attn_bq, L0_attn_Aq, L0_attn_Bq, L0_attn_Wk, L0_attn_bk, L0_attn_Ak,
           L0_attn_Bk, L0_attn_Wv, L0_attn_bv, L0_attn_Av, L0_attn_Bv, L0_attn_Wo, L0_attn_bo, L0_attn_Ao,
           L0_attn_Bo, L0_ffn_Wg, L0_ffn_W1, L0_ffn_W2):
    import numpy as np
    import concourse.bacc as bacc
    from concourse.bass_utils import run_bass_kernel_spmd

    def turned(a):
        return np.ascontiguousarray(np.swapaxes(np.asarray(a), -1, -2))

    def columns(a):
        return turned(np.asarray(a).reshape(-1, 128))

    arrays = {
        "x": np.asarray(x), "xT": turned(x), "ctx": np.asarray(ctx_1024), "ctxT": turned(ctx_1024),
        "WqT": turned(L0_attn_Wq), "WkT": turned(L0_attn_Wk), "WvT": turned(L0_attn_Wv), "WoT": turned(L0_attn_Wo),
        "Aq": np.asarray(L0_attn_Aq), "Ak": np.asarray(L0_attn_Ak), "Av": np.asarray(L0_attn_Av), "Ao": np.asarray(L0_attn_Ao),
        "BqT": turned(L0_attn_Bq), "BkT": turned(L0_attn_Bk), "BvT": turned(L0_attn_Bv), "BoT": turned(L0_attn_Bo),
        "bq": columns(L0_attn_bq), "bk": columns(L0_attn_bk), "bv": np.asarray(L0_attn_bv), "bo": np.asarray(L0_attn_bo),
        "Wg": np.asarray(L0_ffn_Wg), "W1": np.asarray(L0_ffn_W1), "W2": np.asarray(L0_ffn_W2),
    }
    arrays = {"in_" + k: np.ascontiguousarray(a) for k, a in arrays.items()}
    nc = bacc.Bacc("TRN2", target_bir_lowering=False, num_devices=1)
    args = [nc.dram_tensor(k, a.shape, mybir.dt.from_np(a.dtype), kind="ExternalInput").ap() for k, a in arrays.items()]
    out = nc.dram_tensor("out", x.shape, mybir.dt.float32, kind="ExternalOutput").ap()
    decoder_layer(nc, *args, out)
    result = run_bass_kernel_spmd(nc, [arrays], core_ids=[0])
    return result.results[0]["out"]
```
